# Optimizing a Trainium2 kernel written in Bass

```python
import numpy as np
import jax
import jax.numpy as jnp

def _softmax(x, axis=-1):
    return jax.nn.softmax(x, axis=axis)

def _gelu(x):
    return jax.nn.gelu(x, approximate=True)

def _silu(x):
    return jax.nn.silu(x)

def _sigmoid(x):
    return jax.nn.sigmoid(x)

def _layernorm(x, axis=-1, eps=1e-05):
    m = jnp.mean(x, axis=axis, keepdims=True)
    v = jnp.var(x, axis=axis, keepdims=True)
    return (x - m) / jnp.sqrt(v + eps)

def _scatter_add(tgt, idx, src, axis=0):
    return tgt.at[idx].add(src)

def _segment_sum(src, seg, n):
    return jax.ops.segment_sum(src, seg, n)
kernel_name = 'mk_seq_preln_d1_jaxref_r4_9ed6d1'

def setup_inputs(seed: int=0):
    np.random.seed(seed)
    _w = jnp.asarray

    def _L0_attn_setup():
        import jax, jax.numpy as jnp
        import numpy as np
        DIM = 256
        HEADS = 16
        DIM_HEAD = 64
        DIM_INNER = HEADS * DIM_HEAD

        def rms_norm(x, gamma):
            eps = 1e-12
            norm = jnp.maximum(jnp.linalg.norm(x, axis=-1, keepdims=True), eps)
            return x / norm * x.shape[-1] ** 0.5 * (gamma + 1.0)
        key = jax.random.key(seed)
        k1, k2, k3 = jax.random.split(key, 3)
        x = jax.random.normal(k1, (2, 512, DIM), dtype=jnp.float32)
        gamma = jnp.zeros((DIM,), dtype=jnp.float32)
        w_qkv = jax.random.normal(k2, (DIM, DIM_INNER * 3), dtype=jnp.float32) * DIM ** (-0.5)
        w_out = jax.random.normal(k3, (DIM_INNER, DIM), dtype=jnp.float32) * DIM_INNER ** (-0.5)
        return {'x': x, 'gamma': gamma, 'w_qkv': w_qkv, 'w_out': w_out}
    _L0_attn_in = _L0_attn_setup()

    def _L0_ffn_setup():
        import jax, jax.numpy as jnp
        import numpy as np
        NUM_EXPERTS = 8
        TOP_K = 2
        key = jax.random.key(seed)
        ks = jax.random.split(key, 4)
        B, S, H, F = (4, 1024, 256, 1024)
        x = jax.random.normal(ks[0], (B, S, H), dtype=jnp.float32)
        router_w = jax.random.normal(ks[1], (H, NUM_EXPERTS), dtype=jnp.float32) * 0.02
        w1 = jax.random.normal(ks[2], (H, F), dtype=jnp.float32) * 0.02
        b1 = jnp.zeros((F,), dtype=jnp.float32)
        w2 = jax.random.normal(ks[3], (F, H), dtype=jnp.float32) * 0.02
        b2 = jnp.zeros((H,), dtype=jnp.float32)
        return {'x': x, 'router_w': router_w, 'w1': w1, 'b1': b1, 'w2': w2, 'b2': b2}
    _L0_ffn_in = _L0_ffn_setup()
    _d = {'L0_attn_x': _L0_attn_in['x'], 'L0_attn_gamma': _L0_attn_in['gamma'], 'L0_attn_w_qkv': _L0_attn_in['w_qkv'], 'L0_attn_w_out': _L0_attn_in['w_out'], 'L0_ffn_router_w': _L0_ffn_in['router_w'], 'L0_ffn_w1': _L0_ffn_in['w1'], 'L0_ffn_b1': _L0_ffn_in['b1'], 'L0_ffn_w2': _L0_ffn_in['w2'], 'L0_ffn_b2': _L0_ffn_in['b2']}
    _x0 = _d['L0_attn_x']
    _d['L0_attn_x'] = jax.random.normal(jax.random.fold_in(jax.random.key(seed), 1), (8, 512, 256), dtype=_x0.dtype)
    del _x0
    return _d

def reference(L0_attn_x, L0_attn_gamma, L0_attn_w_qkv, L0_attn_w_out, L0_ffn_router_w, L0_ffn_w1, L0_ffn_b1, L0_ffn_w2, L0_ffn_b2):

    def _L0_attn_ref(x, gamma, w_qkv, w_out):
        import jax, jax.numpy as jnp
        import numpy as np
        DIM = 256
        HEADS = 16
        DIM_HEAD = 64
        DIM_INNER = HEADS * DIM_HEAD

        def rms_norm(x, gamma):
            eps = 1e-12
            norm = jnp.maximum(jnp.linalg.norm(x, axis=-1, keepdims=True), eps)
            return x / norm * x.shape[-1] ** 0.5 * (gamma + 1.0)
        b, n, _ = x.shape
        scale = DIM_HEAD ** (-0.5)
        xn = rms_norm(x, gamma)
        qkv = xn @ w_qkv
        qkv = qkv.reshape(b, n, 3, HEADS, DIM_HEAD)
        qkv = jnp.transpose(qkv, (2, 0, 3, 1, 4))
        q, k, v = (qkv[0], qkv[1], qkv[2])
        q = q * scale
        sim = jnp.einsum('bhid,bhjd->bhij', q, k)
        attn = jax.nn.softmax(sim, axis=-1)
        out = jnp.einsum('bhij,bhjd->bhid', attn, v)
        out = jnp.transpose(out, (0, 2, 1, 3)).reshape(b, n, DIM_INNER)
        return out @ w_out

    def _L0_ffn_ref(x, router_w, w1, b1, w2, b2):
        import jax, jax.numpy as jnp
        import numpy as np
        NUM_EXPERTS = 8
        TOP_K = 2
        B, S, H = x.shape
        xt = x.reshape(-1, H)
        router_logits = jnp.matmul(xt, router_w)
        router_probs = jax.nn.softmax(router_logits, axis=-1)
        top_k_probs, top_k_indices = jax.lax.top_k(router_probs, TOP_K)
        top_k_probs = top_k_probs / jnp.sum(top_k_probs, axis=-1, keepdims=True)
        one_hot = jax.nn.one_hot(top_k_indices, NUM_EXPERTS, dtype=xt.dtype)
        combine = jnp.einsum('tk,tke->te', top_k_probs, one_hot)
        expert_out = jnp.matmul(jax.nn.gelu(jnp.matmul(xt, w1) + b1), w2) + b2
        out = expert_out * jnp.sum(combine, axis=-1, keepdims=True)
        return out.reshape(B, S, H)
    x = L0_attn_x
    x = x + _L0_attn_ref(_layernorm(x, axis=-1), L0_attn_gamma, L0_attn_w_qkv, L0_attn_w_out)
    x = x + _L0_ffn_ref(_layernorm(x, axis=-1), L0_ffn_router_w, L0_ffn_w1, L0_ffn_b1, L0_ffn_w2, L0_ffn_b2)
    return x

_drawn_inputs = setup_inputs


def setup_inputs(seed=0):
    import zlib

    import numpy as np

    out = dict(_drawn_inputs(seed))
    spreads = {'L0_attn_gamma': (0.0, 0.416), 'L0_ffn_b1': (0.0, 0.1), 'L0_ffn_b2': (0.0, 0.1)}
    factors = {'L0_ffn_router_w': 8.0}
    for name, (base, spread) in spreads.items():
        noise = np.random.default_rng([zlib.crc32(name.encode()), seed]).standard_normal(out[name].shape)
        drawn = base * np.exp(spread * noise) if base else spread * noise
        out[name] = jnp.asarray(drawn.astype(out[name].dtype))
    for name, factor in factors.items():
        out[name] = (out[name] * factor).astype(out[name].dtype)
    return out
```

```python
from contextlib import ExitStack

import concourse.bass as bass
from concourse import mybir

F32 = mybir.dt.float32
F32R = mybir.dt.float32r
ALU = mybir.AluOpType
ACT = mybir.ActivationFunctionType
AX = mybir.AxisListType

P = 128
B, SEQ, D = 8, 512, 256
HEADS, DH = 16, 64
INNER = HEADS * DH
FF = 1024
EXPERTS = 8
TT = SEQ // P
KT = D // P
FT = FF // P
PAIRS = HEADS // 2
NPAIR = B * PAIRS
NHEAD = B * HEADS
NUNIT = 2 * NHEAD
SPB = 2 * HEADS
LN_EPS = 1e-5
RMS_EPS = 1e-12
SCALE = DH ** -0.5
FIRST_SLOT = -SPB + 16
LAST_SLOT = NUNIT + 11

PS_SCORE = (0, 2)
PS_PT = 4
PS_OUT = 6
PS_AUX = 7
PS_UP = (0, 1)
PS_XT = 2
PS_ROUTER = 4
PS_DOWN = (5, 6)


def plan_aux():
    plan, n_blocks, index = {}, 0, {}
    for slot in range(FIRST_SLOT, LAST_SLOT + 1):
        rel = slot % SPB
        b = slot // SPB
        task = None
        if rel % 4 == 3 and 0 <= (slot + 5) // 4 < NPAIR:
            task = ("q", (slot + 5) // 4)
        elif rel % 4 == 0 and 0 <= (slot + 4) // 4 < NPAIR:
            task = ("k", (slot + 4) // 4)
        elif rel % 8 == 5 and 0 <= (slot + 3) // 8 < NPAIR // 2:
            task = ("v", (slot + 3) // 8, 0)
        elif rel % 8 == 6 and 0 <= (slot + 2) // 8 < NPAIR // 2:
            task = ("v", (slot + 2) // 8, 1)
        elif rel in (25, 26) and 0 <= b + 1 < B:
            task = ("xt", b + 1, rel - 25)
        elif rel in (1, 2) and 0 < b <= B:
            task = ("out", 2 * (b - 1), rel - 1)
        elif rel in (9, 10) and 0 < b <= B:
            task = ("out", 2 * (b - 1) + 1, rel - 9)
        if task:
            plan[slot] = (n_blocks, *task)
            index[task] = n_blocks
            n_blocks += 1
    return plan, index


def layer_kernel(nc, x, gamma_cols, w_qkv, w_out, router_w, w1, b1_cols, w2, b2_rows, ident, out):
    aux_at, aux_index = plan_aux()
    x_v = x.rearrange("b (p t) d -> b p t d", t=TT)
    out_v = out.rearrange("b (p t) d -> b p t d", t=TT)
    x1_dram = nc.dram_tensor("x1_scratch", (B, P, TT, D), F32, kind="Internal").ap()
    wqkv_v = w_qkv.rearrange("(k p) n -> p k n", p=P)
    wout_v = w_out.rearrange("(k p) n -> p k n", p=P)
    w1_v = w1.rearrange("(k p) n -> p k n", p=P)
    w2_v = w2.rearrange("(k p) n -> p k n", p=P)
    rw_v = router_w.rearrange("(k p) e -> p k e", p=P)

    with ExitStack() as ctx:
        def sb(name, shape, dt, scope=ctx):
            return scope.enter_context(nc.sbuf_tensor(name, shape, dt))

        def sem(name):
            return ctx.enter_context(nc.semaphore(name))

        ps = ctx.enter_context(nc.psum_tensor("ps", [P, 8, 512], F32))

        wbig = [sb("wbig_hi", [P, KT * 3 * INNER], F32R), sb("wbig_lo", [P, KT * 3 * INNER], F32R)]
        wqkv = [w[:, :].rearrange("p (k n) -> p k n", k=KT) for w in wbig]
        w1s = [w[:, 0:KT * FF].rearrange("p (k n) -> p k n", k=KT) for w in wbig]
        w2s = [w[:, KT * FF:KT * FF + FT * D].rearrange("p (k n) -> p k n", k=FT) for w in wbig]
        identity = sb("identity", [P, P], F32)
        gain = sb("gain", [P, KT], F32)
        gamma_sb = sb("gamma_sb", [P, KT], F32)
        b1_sb = sb("b1_sb", [P, FT], F32)
        rw_sb = sb("rw_sb", [P, KT, EXPERTS], F32)
        rw_parts = sb("rw_parts", [P, KT, 2 * EXPERTS], F32R)
        half_pos = sb("half_pos", [P, TT], F32)
        half_neg = sb("half_neg", [P, TT], F32)
        ln_stats = sb("ln_stats", [P, TT, 6], F32)
        ln_mv = sb("ln_mv", [P, TT, 2], F32)
        ln_veps = sb("ln_veps", [P, TT], F32)
        ln_std = sb("ln_std", [P, TT], F32)
        ln_rstd = sb("ln_rstd", [P, TT], F32)
        ln_norm = sb("ln_norm", [P, 3, TT], F32)
        ln_scale = sb("ln_scale", [P, TT], F32)
        wstage = sb("wstage", [P, 1024], F32)

        att = ctx.enter_context(ExitStack())
        wout = [sb("wout_hi", [P, PAIRS, D], F32R, att), sb("wout_lo", [P, PAIRS, D], F32R, att)]
        xbuf = sb("xbuf", [P, 2, TT, D], F32, att)
        xn = sb("xn", [P, TT, D], F32, att)
        xT = [sb("xT_hi", [P, KT, SEQ], F32R, att), sb("xT_lo", [P, KT, SEQ], F32R, att)]
        QL, QH, KH, KL = range(4)
        nat = sb("nat", [P, 4, SEQ], F32R, att)
        NSTACK = 3
        stack = sb("stack", [P, NSTACK, 3, SEQ], F32R, att)
        vbuf = sb("vbuf", [P, 2, TT, 4, 2 * DH], F32R, att)
        NPROB = 3
        prob = sb("prob", [P, NPROB, 1024], F32, att)
        pT = [sb("pT_hi", [P, 2, TT, SEQ], F32R, att), sb("pT_lo", [P, 2, TT, SEQ], F32R, att)]
        vlo_part = sb("vlo_part", [DH, SEQ], F32, att)
        att32 = sb("att32", [P, SEQ], F32, att)
        NATT = 7
        attT = [sb("attT_hi", [P, NATT, SEQ], F32R, att), sb("attT_lo", [P, NATT, SEQ], F32R, att)]
        negmax = sb("negmax", [P, 4, 2], F32, att)
        rowsum = sb("rowsum", [P, 4, 2], F32, att)
        rowinv = sb("rowinv", [P, 4, 2], F32, att)
        att.close()

        ffn = ctx.enter_context(ExitStack())
        f_x1 = sb("f_x1", [P, 3, TT, D], F32, ffn)
        b2_sb = sb("b2_sb", [P, D], F32, ffn)
        f_x2 = sb("f_x2", [P, TT, D], F32, ffn)
        f_xT = [sb("f_xT_hi", [P, 2, KT, SEQ], F32R, ffn), sb("f_xT_lo", [P, 2, KT, SEQ], F32R, ffn)]
        f_h = sb("f_h", [P, 3, SEQ], F32, ffn)
        f_hT = [sb("f_hT_hi", [P, FT, SEQ], F32R, ffn), sb("f_hT_lo", [P, FT, SEQ], F32R, ffn)]
        f_y = sb("f_y", [P, 2, 2, D], F32, ffn)
        f_o = sb("f_o", [P, 2, TT, D], F32, ffn)
        r_half = sb("r_half", [P, TT, EXPERTS], F32, ffn)
        r_logit = sb("r_logit", [P, TT, EXPERTS], F32, ffn)
        r_max = sb("r_max", [P, TT], F32, ffn)
        r_shift = sb("r_shift", [P, TT, EXPERTS], F32, ffn)
        r_exp = sb("r_exp", [P, TT, EXPERTS], F32, ffn)
        r_sum = sb("r_sum", [P, TT], F32, ffn)
        r_inv = sb("r_inv", [P, TT], F32, ffn)
        r_prob = sb("r_prob", [P, TT, EXPERTS], F32, ffn)
        r_top = sb("r_top", [P, TT, 8], F32, ffn)
        r_tsum = sb("r_tsum", [P, TT], F32, ffn)
        r_tinv = sb("r_tinv", [P, TT], F32, ffn)
        r_pair = sb("r_pair", [P, TT, 2], F32, ffn)
        r_weight = sb("r_weight", [P, 2, TT], F32, ffn)
        ffn.close()

        s_const = sem("const_loaded")
        s_b2 = sem("b2_loaded")
        s_x = [sem(f"x_loaded{i}") for i in range(2)]
        s_wload = [sem(f"weights_loaded{i}") for i in range(3)]
        s_wstage = sem("ffn_weights_loaded")
        s_whi = sem("weights_hi")
        s_wlo = sem("weights_lo")
        s_half = sem("exponents_set")
        s_dve = sem("dve_step")
        s_var = sem("variance_ready")
        s_pow = sem("powers_ready")
        s_xn = sem("xn_ready")
        s_score = sem("scores_done")
        s_max = sem("rowmax_done")
        s_exp = sem("exp_done")
        s_inv = sem("rowinv_done")
        s_prob = sem("probabilities_normalised")
        s_pt = sem("probabilities_transposed")
        s_pthi = sem("pT_hi_done")
        s_ptlo = sem("pT_lo_done")
        s_pv = sem("pv_done")
        s_vlo = sem("vlo_part_copied")
        s_head = sem("head_output_done")
        s_atthi = sem("attT_hi_done")
        s_att = sem("attT_done")
        s_auxfull = sem("aux_block_in_psum")
        s_auxhi = sem("aux_hi_done")
        s_aux = sem("aux_block_done")
        s_stack = [sem(f"head_stacked{i}") for i in range(NSTACK)]
        s_x1 = sem("x1_stored")
        s_fx1 = [sem(f"f_x1_loaded{i}") for i in range(3)]
        s_fx2 = sem("f_x2_ready")
        s_fxt = sem("f_x2_transposed")
        s_fxthi = sem("f_xT_hi")
        s_fxtlo = sem("f_xT_lo")
        s_frt = sem("router_logits")
        s_frs = sem("router_shifted")
        s_fre = sem("router_exp")
        s_frw = sem("router_weight")
        s_up = sem("up_done")
        s_gelu = sem("gelu_done")
        s_hhi = sem("hidden_hi")
        s_hlo = sem("hidden_lo")
        s_down = sem("down_done")
        s_fy = sem("down_read")
        s_fo = sem("ffn_out_ready")
        s_out = [sem(f"out_stored{i}") for i in range(2)]

        block = ctx.enter_context(nc.Block())

        N_CONST = 5
        N_ATT_CHUNKS = 8
        N_CHUNKS = 12
        all_aux = len(aux_at)

        def weight_chunk(i):
            if i < 6:
                cols, k = i // 2, i % 2
                c = slice(cols * INNER, (cols + 1) * INNER)
                return wqkv_v[:, k, c], [w[:, k, c] for w in wqkv]
            if i < 8:
                c = slice((i - 6) * 4, (i - 6) * 4 + 4)
                return wout_v[:, c, :], [w[:, c, :].rearrange("p k n -> p (k n)") for w in wout]
            if i < 10:
                return w1_v[:, i - 8, :], [w[:, i - 8, :] for w in w1s]
            c = slice((i - 10) * 4, (i - 10) * 4 + 4)
            return w2_v[:, c, :], [w[:, c, :].rearrange("p k n -> p (k n)") for w in w2s]

        def weight_stage(i):
            return prob[:, i % NPROB, :] if i < N_ATT_CHUNKS else wstage[:, :]

        def wait_weight_loaded(eng, i):
            if i < N_ATT_CHUNKS:
                eng.wait_ge(s_wload[i % NPROB], 16 * (i // NPROB + 1))
            else:
                eng.wait_ge(s_wstage, 16 * (i - N_ATT_CHUNKS + 1))

        def weight_slots(slot):
            if slot == -8:
                return range(N_ATT_CHUNKS)
            if NUNIT - 6 <= slot < NUNIT - 2:
                return [N_ATT_CHUNKS + slot - (NUNIT - 6)]
            return []

        def ln_task(slot):
            b, step = divmod(slot - 17, SPB)
            return (b + 1, step) if step < 7 and 0 <= b + 1 < B else None

        def stack_loads_before(slot_of_stack, head):
            return 48 * (head // NSTACK + 1)

        def wait_attention_done(eng):
            eng.wait_ge(s_aux, all_aux)
            eng.wait_ge(s_x1, 16 * B)

        @block.sync
        def _(sp):
            sp.dma_start(xbuf[:, 0], x_v[0]).then_inc(s_x[0], 16)
            sp.dma_start(identity[:, :], ident).then_inc(s_const, 16)
            sp.dma_start(gamma_sb[:, :], gamma_cols).then_inc(s_const, 16)
            sp.dma_start(b1_sb[:, :], b1_cols).then_inc(s_const, 16)
            for k in range(KT):
                sp.dma_start(rw_sb[:, k, :], rw_v[:, k, :]).then_inc(s_const, 16)
            for i in range(N_ATT_CHUNKS):
                if i >= NPROB:
                    sp.wait_ge(s_wlo, i - NPROB + 1)
                sp.dma_start(weight_stage(i), weight_chunk(i)[0]).then_inc(s_wload[i % NPROB], 16)

            for slot in range(FIRST_SLOT, LAST_SLOT + 1):
                b, rel = divmod(slot, SPB)
                if rel == 11 and 0 <= b - 1 < B:
                    sp.wait_ge(s_aux, aux_index[("out", 2 * (b - 1) + 1, 1)] + 1)
                    sp.dma_start(x1_dram[b - 1], xbuf[:, (b - 1) % 2]).then_inc(s_x1, 16)
                if rel == 12 and 1 <= b + 1 < B:
                    if b >= 1:
                        sp.wait_ge(s_x1, 16 * b)
                    sp.dma_start(xbuf[:, (b + 1) % 2], x_v[b + 1]).then_inc(s_x[(b + 1) % 2], 16)
                pair = (slot + 3) // 4
                if rel % 4 == 1 and 0 <= pair < NPAIR:
                    sp.wait_ge(s_aux, aux_index[("k", pair)] + 1)
                    for odd in range(2):
                        head = 2 * pair + odd
                        i = head % NSTACK
                        src = nat[odd * DH:(odd + 1) * DH].bitcast(F32)
                        dst = stack[:, i].bitcast(F32)
                        if head >= NSTACK:
                            sp.wait_ge(s_score, 2 * (head - NSTACK) + 2)
                        sp.dma_start(dst[0:DH, 0:3, :], src[:, QH:KL + 1, :]).then_inc(s_stack[i], 16)
                        sp.dma_start(dst[DH:P, 0:1, :], src[:, QL:QL + 1, :]).then_inc(s_stack[i], 16)
                        sp.dma_start(dst[DH:P, 1:3, :], src[:, KH:KL + 1, :]).then_inc(s_stack[i], 16)
                for i in weight_slots(slot):
                    if i >= N_ATT_CHUNKS:
                        if i > N_ATT_CHUNKS:
                            sp.wait_ge(s_wlo, i)
                        sp.dma_start(weight_stage(i), weight_chunk(i)[0]).then_inc(s_wstage, 16)

            wait_attention_done(sp)
            sp.dma_start(b2_sb[:, :], b2_rows).then_inc(s_b2, 16)
            for c in range(B):
                if c >= 3:
                    sp.wait_ge(s_fo, c - 2)
                sp.dma_start(f_x1[:, c % 3], x1_dram[c]).then_inc(s_fx1[c % 3], 16)
                if c >= 2:
                    sp.wait_ge(s_fo, c - 1)
                    sp.dma_start(out_v[c - 2], f_o[:, (c - 2) % 2]).then_inc(s_out[(c - 2) % 2], 16)
            for c in range(B - 2, B):
                sp.wait_ge(s_fo, c + 1)
                sp.dma_start(out_v[c], f_o[:, c % 2]).then_inc(s_out[c % 2], 16)
            for i in range(2):
                sp.wait_ge(s_out[i], 16 * (B // 2))

        @block.tensor
        def _(pe):
            def products(dst, stationary, moving, first, last):
                terms = [(0, 0), (1, 0), (0, 1)]
                for n, (i, j) in enumerate(terms):
                    ins = pe.matmul(dst, stationary[i], moving[j], start=first and n == 0,
                                    stop=last and n == len(terms) - 1)
                return ins

            def scores(n):
                head, half = divmod(n, 2)
                i = head % NSTACK
                if half == 0:
                    pe.wait_ge(s_stack[i], stack_loads_before(i, head))
                if n >= 2:
                    pe.wait_ge(s_exp, n - 1)
                for j in range(2):
                    q0 = (2 * half + j) * P
                    dst = ps[:, PS_SCORE[n % 2] + j, :]
                    pe.matmul(dst, stack[:, i, 0, q0:q0 + P], stack[:, i, 1, :], start=True, stop=False)
                    ins = pe.matmul(dst, stack[:, i, 0, q0:q0 + P], stack[:, i, 2, :], start=False, stop=True)
                ins.then_inc(s_score, 1)

            def transpose_prob(n):
                pe.wait_ge(s_prob, n + 1)
                if n >= 1:
                    pe.wait_ge(s_ptlo, n)
                for j in range(2):
                    for k in range(TT):
                        ins = pe.transpose(ps[:, PS_PT + j, k * P:(k + 1) * P],
                                           prob[:, n % NPROB, j * SEQ + k * P:j * SEQ + (k + 1) * P],
                                           identity[:, :])
                ins.then_inc(s_pt, 1)

            def weighted_values(head, part):
                quad = head // 4
                if part == 0:
                    pe.wait_ge(s_ptlo, 2 * head + 2)
                    pe.wait_ge(s_aux, aux_index[("v", quad, 1)] + 1)
                    if head >= 1:
                        pe.wait_ge(s_head, head)
                for k in range(TT):
                    ins = pe.matmul(ps[:, PS_OUT, :], vbuf[:, quad % 2, k, head % 4, :],
                                    pT[part][:, head % 2, k, :], start=part == 0 and k == 0,
                                    stop=part == 1 and k == TT - 1)
                if part == 1:
                    ins.then_inc(s_pv, 1)

            def aux(block_no, kind, *args):
                if block_no >= 1:
                    pe.wait_ge(s_aux, block_no)
                bank = ps[:, PS_AUX, :]
                if kind == "xt":
                    b, k = args
                    pe.wait_ge(s_xn, b + 1)
                    if b == 0:
                        pe.wait_ge(s_const, 16 * N_CONST)
                    for t in range(TT):
                        ins = pe.transpose(bank[:, t * P:(t + 1) * P], xn[:, t, k * P:(k + 1) * P],
                                           identity[:, :])
                elif kind in "qk":
                    pair, = args
                    base = (kind == "k") * INNER + pair % PAIRS * P
                    pe.wait_ge(s_wlo, 2 if kind == "q" else 4)
                    for k in range(KT):
                        ins = products(bank, [w[:, k, base:base + P] for w in wqkv],
                                       [v[:, k, :] for v in xT], k == 0, k == KT - 1)
                elif kind == "v":
                    quad, part = args
                    base = 2 * INNER + quad % (PAIRS // 2) * 4 * DH
                    pe.wait_ge(s_wlo, 6)
                    for t in range(2):
                        c = (2 * part + t) * P
                        for k in range(KT):
                            ins = products(bank[:, t * D:(t + 1) * D], [v[:, k, c:c + P] for v in xT],
                                           [w[:, k, base:base + 4 * DH] for w in wqkv], k == 0, k == KT - 1)
                elif kind == "out":
                    half, part = args
                    pe.wait_ge(s_wlo, 8)
                    pe.wait_ge(s_att, 4 * half + 4)
                    for t in range(2):
                        c = (2 * part + t) * P
                        for j in range(4):
                            pair = 4 * half + j
                            ins = products(bank[:, t * D:(t + 1) * D],
                                           [a[:, pair % NATT, c:c + P] for a in attT],
                                           [w[:, pair % PAIRS, :] for w in wout], j == 0, j == 3)
                ins.then_inc(s_auxfull, 1)

            for slot in range(FIRST_SLOT, LAST_SLOT + 1):
                if 0 <= slot < NUNIT:
                    scores(slot)
                if slot in aux_at:
                    aux(*aux_at[slot])
                if 0 <= slot - 2 < NUNIT:
                    transpose_prob(slot - 2)
                if 0 <= (slot - 4) // 2 < NHEAD:
                    weighted_values(*divmod(slot - 4, 2))

            wait_attention_done(pe)
            pe.wait_ge(s_wlo, N_CHUNKS)

            def transpose_and_route(c):
                pe.wait_ge(s_fx2, c + 1)
                if c >= 1:
                    pe.wait_ge(s_fxtlo, c)
                for k in range(KT):
                    for t in range(TT):
                        ins = pe.transpose(ps[:, PS_XT + k, t * P:(t + 1) * P],
                                           f_x2[:, t, k * P:(k + 1) * P], identity[:, :])
                ins.then_inc(s_fxt, 1)
                pe.wait_ge(s_fxtlo, c + 1)
                if c >= 1:
                    pe.wait_ge(s_frs, c)
                for t in range(TT):
                    for k in range(KT):
                        for part in range(2):
                            ins = pe.matmul(ps[:, PS_ROUTER, t * 16:(t + 1) * 16],
                                            f_xT[part][:, c % 2, k, t * P:(t + 1) * P], rw_parts[:, k, :],
                                            start=k == 0 and part == 0, stop=k == KT - 1 and part == 1)
                ins.then_inc(s_frt, 1)

            def up(c):
                for f in range(FT):
                    n = c * FT + f
                    if n >= 2:
                        pe.wait_ge(s_gelu, n - 1)
                    for k in range(KT):
                        ins = products(ps[:, PS_UP[n % 2], :], [w[:, k, f * P:(f + 1) * P] for w in w1s],
                                       [v[:, c % 2, k, :] for v in f_xT], k == 0, k == KT - 1)
                    ins.then_inc(s_up, 1)

            def down(c):
                for part in range(2):
                    if c >= 1:
                        pe.wait_ge(s_fy, 2 * (c - 1) + part + 1)
                    for t in range(2):
                        q = (2 * part + t) * P
                        for f in range(FT):
                            pe.wait_ge(s_hlo, c * FT + f + 1)
                            ins = products(ps[:, PS_DOWN[part], t * D:(t + 1) * D],
                                           [h[:, f, q:q + P] for h in f_hT],
                                           [w[:, f, :] for w in w2s], f == 0, f == FT - 1)
                    ins.then_inc(s_down, 1)

            transpose_and_route(0)
            for c in range(B):
                up(c)
                if c + 1 < B:
                    transpose_and_route(c + 1)
                down(c)

        @block.scalar
        def _(act):
            def aux_hi(block_no, kind, *args):
                act.wait_ge(s_auxfull, block_no + 1)
                bank = ps[:, PS_AUX, :]
                if kind == "xt":
                    ins = act.activation(xT[0][:, args[1], :], bank, ACT.Copy, scale=gain[:, args[1]:args[1] + 1])
                elif kind == "q":
                    pair, = args
                    for head in (2 * pair - 2, 2 * pair - 1):
                        if head >= 0:
                            act.wait_ge(s_stack[head % NSTACK], stack_loads_before(head % NSTACK, head))
                    ins = act.activation(nat[:, QH, :], bank, ACT.Copy, scale=SCALE)
                elif kind == "k":
                    ins = act.activation(nat[:, KH, :], bank, ACT.Copy)
                elif kind == "v":
                    quad, part = args
                    ins = act.activation(vbuf[:, quad % 2, 2 * part:2 * part + 2, :, 0:DH],
                                         bank.rearrange("p (t h d) -> p t h d", t=2, h=4), ACT.Copy)
                ins.then_inc(s_auxhi, 1)

            for slot in range(FIRST_SLOT, LAST_SLOT + 1):
                for i in weight_slots(slot):
                    wait_weight_loaded(act, i)
                    act.activation(weight_chunk(i)[1][0], weight_stage(i), ACT.Copy).then_inc(s_whi, 1)
                if slot in aux_at and aux_at[slot][1] != "out":
                    aux_hi(*aux_at[slot])
                n = slot - 2
                if 0 <= n < NUNIT:
                    head, half = divmod(n, 2)
                    act.wait_ge(s_pt, n + 1)
                    dst = pT[0][:, head % 2, :, half * 2 * P:(half + 1) * 2 * P]
                    act.activation(dst.rearrange("p k (j q) -> p j k q", j=2),
                                   ps[:, PS_PT:PS_PT + 2, :].rearrange("p j (k q) -> p j k q", k=TT),
                                   ACT.Copy).then_inc(s_pthi, 1)
                n = slot
                if 0 <= n < NUNIT:
                    act.wait_ge(s_max, n + 1)
                    if n >= NPROB:
                        act.wait_ge(s_pt, n - NPROB + 1)
                    for j in range(2):
                        ins = act.activation(prob[:, n % NPROB, j * SEQ:(j + 1) * SEQ],
                                             ps[:, PS_SCORE[n % 2] + j, :], ACT.Exp,
                                             bias=negmax[:, n % 4, j:j + 1], accum_out=rowsum[:, n % 4, j:j + 1])
                    ins.then_inc(s_exp, 1)
                head, part = divmod(slot - 4, 2)
                if part == 1 and 0 <= head < NHEAD:
                    act.wait_ge(s_pv, head + 1)
                    act.activation(vlo_part[:, :], ps[DH:P, PS_OUT, :], ACT.Copy).then_inc(s_vlo, 1)

            wait_attention_done(act)

            def ffn_prep(c):
                act.wait_ge(s_fxt, c + 1)
                act.activation(f_xT[0][:, c % 2], ps[:, PS_XT:PS_XT + 2, :], ACT.Copy).then_inc(s_fxthi, 1)
                act.wait_ge(s_frs, c + 1)
                act.activation(r_exp[:, :, :], r_shift[:, :, :], ACT.Exp).then_inc(s_fre, 1)

            ffn_prep(0)
            for c in range(B):
                for f in range(FT):
                    n = c * FT + f
                    act.wait_ge(s_up, n + 1)
                    if n >= 3:
                        act.wait_ge(s_hlo, n - 2)
                    act.activation(f_h[:, n % 3, :], ps[:, PS_UP[n % 2], :], ACT.Gelu_apprx_tanh,
                                   bias=b1_sb[:, f:f + 1]).then_inc(s_gelu, 1)
                if c + 1 < B:
                    ffn_prep(c + 1)

        @block.gpsimd
        def _(pool):
            pool.memset(half_pos[:, :], 0.5).then_inc(s_half, 1)
            pool.memset(half_neg[:, :], -0.5).then_inc(s_half, 1)
            pool.wait_ge(s_half, 2)

            def powers(n):
                pool.wait_ge(s_var, n + 1)
                pool.tensor_tensor(ln_std[:, :], ln_mv[:, :, 1], half_pos[:, :], ALU.pow)
                pool.tensor_tensor(ln_rstd[:, :], ln_veps[:, :], half_neg[:, :], ALU.pow).then_inc(s_pow, 1)

            def times(dst, src, scalar):
                return pool.tensor_scalar(dst, src, scalar, 1.0, ALU.mult, ALU.mult)

            for slot in range(FIRST_SLOT, LAST_SLOT + 1):
                n = slot - 1
                if 0 <= n < NUNIT:
                    pool.wait_ge(s_inv, n + 1)
                    for j in range(2):
                        p = prob[:, n % NPROB, j * SEQ:(j + 1) * SEQ]
                        ins = times(p, p, rowinv[:, n % 4, j:j + 1])
                    ins.then_inc(s_prob, 1)
                task = ln_task(slot)
                if task and task[1] == 4:
                    powers(task[0])
                pair, r = divmod(slot - 8, 4)
                if r == 0 and 0 <= pair < NPAIR:
                    pool.wait_ge(s_head, 2 * pair + 2)
                    if pair >= NATT:
                        pool.wait_ge(s_aux, aux_index[("out", (pair - NATT) // 4, 1)] + 1)
                    pool.tensor_scalar(attT[0][:, pair % NATT, :], att32[:, :], 1.0, 1.0, ALU.mult, ALU.mult)\
                        .then_inc(s_atthi, 1)
                    pool.wait_ge(s_atthi, pair + 1)
                    pool.tensor_tensor(attT[1][:, pair % NATT, :], att32[:, :], attT[0][:, pair % NATT, :],
                                       ALU.subtract).then_inc(s_att, 1)

            wait_attention_done(pool)
            powers(B)
            for c in range(B):
                for f in range(FT):
                    n = c * FT + f
                    pool.wait_ge(s_gelu, n + 1)
                    if c >= 1 and f == 0:
                        pool.wait_ge(s_down, 2 * c)
                    pool.tensor_scalar(f_hT[0][:, f, :], f_h[:, n % 3, :], 1.0, 1.0, ALU.mult, ALU.mult)\
                        .then_inc(s_hhi, 1)
                    if f == 3 and c + 1 < B:
                        powers(B + c + 1)

        @block.vector
        def _(dve):
            chain = [0]

            def link(ins):
                chain[0] += 1
                ins.then_inc(s_dve, 1)
                dve.wait_ge(s_dve, chain[0])

            def statistics_step(src, t, last):
                link(dve.bn_stats(ln_stats[:, t, :], src))
                link(dve.bn_aggr(ln_mv[:, t, :], ln_stats[:, t, :]))
                if last:
                    dve.tensor_scalar(ln_veps[:, :], ln_mv[:, :, 1], LN_EPS, None, ALU.add).then_inc(s_var, 1)

            def attention_scale():
                root = float(D) ** 0.5
                link(dve.scalar_tensor_tensor(ln_norm[:, 0, :], ln_std[:, :], root, ln_rstd[:, :],
                                              ALU.mult, ALU.mult))
                link(dve.tensor_scalar(ln_norm[:, 1, :], ln_norm[:, 0, :], RMS_EPS, None, ALU.max))
                link(dve.reciprocal(ln_norm[:, 2, :], ln_norm[:, 1, :]))
                link(dve.scalar_tensor_tensor(ln_scale[:, :], ln_rstd[:, :], root, ln_norm[:, 2, :],
                                              ALU.mult, ALU.mult))

            def normalise(dst, src, t, scale):
                return dve.tensor_scalar(dst, src, ln_mv[:, t, 0:1], scale[:, t:t + 1], ALU.subtract, ALU.mult)

            def lo(dst, full, hi, scale=None):
                if scale is None:
                    return dve.tensor_tensor(dst, full, hi, ALU.subtract)
                return dve.scalar_tensor_tensor(dst, full, scale, hi, ALU.mult, ALU.subtract)

            def aux_done(block_no, kind, *args):
                bank = ps[:, PS_AUX, :]
                if kind == "out":
                    half, part = args
                    dve.wait_ge(s_auxfull, block_no + 1)
                    if half % 2 == 1:
                        dve.wait_ge(s_aux, aux_index[("out", half - 1, 1)] + 1)
                    dst = xbuf[:, half // 2 % 2, 2 * part:2 * part + 2, :].rearrange("p t d -> p (t d)")
                    dve.tensor_tensor(dst, bank, dst, ALU.add).then_inc(s_aux, 1)
                    return
                hi_no = sum(1 for k in range(block_no + 1) if aux_kind[k] != "out")
                dve.wait_ge(s_auxhi, hi_no)
                if kind == "xt":
                    k = args[1]
                    ins = lo(xT[1][:, k, :], bank, xT[0][:, k, :], gain[:, k:k + 1])
                elif kind == "q":
                    ins = lo(nat[:, QL, :], bank, nat[:, QH, :], SCALE)
                elif kind == "k":
                    ins = lo(nat[:, KL, :], bank, nat[:, KH, :])
                else:
                    quad, part = args
                    v = vbuf[:, quad % 2, 2 * part:2 * part + 2, :, :]
                    ins = lo(v[:, :, :, DH:2 * DH], bank.rearrange("p (t h d) -> p t h d", t=2, h=4),
                             v[:, :, :, 0:DH])
                ins.then_inc(s_aux, 1)

            aux_kind = [t[1] for t in sorted(aux_at.values())]

            for slot in range(FIRST_SLOT, LAST_SLOT + 1):
                n = slot
                if 0 <= n < NUNIT:
                    dve.wait_ge(s_score, n + 1)
                    dve.tensor_reduce(negmax[:, n % 4, :], ps[:, PS_SCORE[n % 2]:PS_SCORE[n % 2] + 2, :],
                                      AX.X, ALU.max, negate=True).then_inc(s_max, 1)
                n = slot - 1
                if 0 <= n < NUNIT:
                    dve.wait_ge(s_exp, n + 1)
                    dve.reciprocal(rowinv[:, n % 4, :], rowsum[:, n % 4, :]).then_inc(s_inv, 1)
                head, part = divmod(slot - 6, 2)
                if part == 0 and 0 <= head < NHEAD:
                    dve.wait_ge(s_vlo, head + 1)
                    if head >= 2 and head % 2 == 0:
                        dve.wait_ge(s_att, head // 2)
                    dve.tensor_tensor(att32[head % 2 * DH:(head % 2 + 1) * DH, :], ps[0:DH, PS_OUT, :],
                                      vlo_part[:, :], ALU.add).then_inc(s_head, 1)
                if slot in aux_at:
                    aux_done(*aux_at[slot])
                n = slot - 2
                if 0 <= n < NUNIT:
                    head, half = divmod(n, 2)
                    dve.wait_ge(s_pthi, n + 1)
                    part = [p[:, head % 2, :, half * 2 * P:(half + 1) * 2 * P].rearrange(
                        "p k (j q) -> p j k q", j=2) for p in pT]
                    lo(part[1], ps[:, PS_PT:PS_PT + 2, :].rearrange("p j (k q) -> p j k q", k=TT),
                       part[0]).then_inc(s_ptlo, 1)
                for i in weight_slots(slot):
                    if i == 0:
                        dve.wait_ge(s_const, 16 * N_CONST)
                        dve.tensor_scalar(gain[:, :], gamma_sb[:, :], 1.0, None, ALU.add)
                        link(dve.tensor_copy(rw_parts[:, :, 0:EXPERTS], rw_sb[:, :, :]))
                        link(lo(rw_parts[:, :, EXPERTS:], rw_sb[:, :, :], rw_parts[:, :, 0:EXPERTS]))
                    dve.wait_ge(s_whi, i + 1)
                    hi_part, lo_part = weight_chunk(i)[1]
                    lo(lo_part, weight_stage(i), hi_part).then_inc(s_wlo, 1)
                task = ln_task(slot)
                if task:
                    b, step = task
                    xb = xbuf[:, b % 2]
                    if step == 0:
                        dve.wait_ge(s_x[b % 2], 16 * (b // 2 + 1))
                    if step < 4:
                        statistics_step(xb[:, step, :], step, step == 3)
                    elif step == 5:
                        dve.wait_ge(s_pow, b + 1)
                        attention_scale()
                    elif step == 6:
                        for t in range(TT):
                            ins = normalise(xn[:, t, :], xb[:, t, :], t, ln_scale)
                        ins.then_inc(s_xn, 1)

            wait_attention_done(dve)

            def ffn_stats(c, t):
                if t == 0:
                    dve.wait_ge(s_fx1[c % 3], 16 * (c // 3 + 1))
                statistics_step(f_x1[:, c % 3, t, :], t, t == TT - 1)

            def ffn_normalise(c):
                dve.wait_ge(s_pow, B + c + 1)
                for t in range(TT):
                    ins = normalise(f_x2[:, t, :], f_x1[:, c % 3, t, :], t, ln_rstd)
                ins.then_inc(s_fx2, 1)

            def ffn_split(c):
                dve.wait_ge(s_fxthi, c + 1)
                lo(f_xT[1][:, c % 2], ps[:, PS_XT:PS_XT + 2, :], f_xT[0][:, c % 2]).then_inc(s_fxtlo, 1)

            def route(c):
                wide = (P, TT, EXPERTS)
                logits = ps[:, PS_ROUTER, 0:TT * 16].rearrange("p (t e) -> p t e", t=TT)
                dve.wait_ge(s_frt, c + 1)
                link(dve.tensor_copy(r_half[:, :, :], logits[:, :, EXPERTS:]))
                link(dve.tensor_tensor(r_logit[:, :, :], logits[:, :, 0:EXPERTS], r_half[:, :, :], ALU.add))
                link(dve.tensor_reduce(r_max[:, :], r_logit[:, :, :], AX.X, ALU.max))
                dve.tensor_tensor(r_shift[:, :, :], r_logit[:, :, :],
                                  r_max[:, :].unsqueeze(2).broadcast_to(wide), ALU.subtract).then_inc(s_frs, 1)
                dve.wait_ge(s_fre, c + 1)
                link(dve.reduce_sum(r_sum[:, :], r_exp[:, :, :], AX.X))
                link(dve.reciprocal(r_inv[:, :], r_sum[:, :]))
                link(dve.tensor_tensor(r_prob[:, :, :], r_exp[:, :, :],
                                       r_inv[:, :].unsqueeze(2).broadcast_to(wide), ALU.mult))
                for t in range(TT):
                    ins = dve.max(r_top[:, t, :], r_prob[:, t, :])
                link(ins)
                link(dve.tensor_tensor(r_tsum[:, :], r_top[:, :, 0], r_top[:, :, 1], ALU.add))
                link(dve.reciprocal(r_tinv[:, :], r_tsum[:, :]))
                link(dve.tensor_tensor(r_pair[:, :, :], r_top[:, :, 0:2],
                                       r_tinv[:, :].unsqueeze(2).broadcast_to((P, TT, 2)), ALU.mult))
                link(dve.tensor_tensor(r_weight[:, c % 2, :], r_pair[:, :, 0], r_pair[:, :, 1], ALU.add))

            def finish(c):
                if c == 0:
                    dve.wait_ge(s_b2, 16)
                for part in range(2):
                    n = 2 * c + part
                    dve.wait_ge(s_down, n + 1)
                    y = f_y[:, part]
                    link(dve.tensor_tensor(y, ps[:, PS_DOWN[part], :].rearrange("p (t d) -> p t d", t=2),
                                           b2_sb[:, :].unsqueeze(1).broadcast_to((P, 2, D)), ALU.add))
                    if part == 0 and c >= 2:
                        dve.wait_ge(s_out[c % 2], 16 * (c // 2))
                    for t in range(2):
                        tile = 2 * part + t
                        ins = dve.scalar_tensor_tensor(f_o[:, c % 2, tile, :], y[:, t, :],
                                                       r_weight[:, c % 2, tile:tile + 1],
                                                       f_x1[:, c % 3, tile, :], ALU.mult, ALU.add)
                        if t == 0:
                            ins.then_inc(s_fy, 1)
                    if part == 1:
                        ins.then_inc(s_fo, 1)

            for t in range(TT):
                ffn_stats(0, t)
            ffn_normalise(0)
            ffn_split(0)
            route(0)
            for c in range(B):
                for f in range(FT):
                    n = c * FT + f
                    dve.wait_ge(s_hhi, n + 1)
                    lo(f_hT[1][:, f, :], f_h[:, n % 3, :], f_hT[0][:, f, :]).then_inc(s_hlo, 1)
                    if c + 1 < B:
                        if f < 4:
                            ffn_stats(c + 1, f)
                        elif f == 5:
                            ffn_normalise(c + 1)
                if c + 1 < B:
                    ffn_split(c + 1)
                    route(c + 1)
                finish(c)


def kernel(**inputs):
    import numpy as np
    import concourse.bacc as bacc
    from concourse.bass_utils import run_bass_kernel_spmd

    get = lambda name: np.asarray(inputs[name])
    arrays = {
        "x": get("L0_attn_x"),
        "gamma_cols": np.ascontiguousarray(get("L0_attn_gamma").reshape(KT, P).T),
        "w_qkv": get("L0_attn_w_qkv"),
        "w_out": get("L0_attn_w_out"),
        "router_w": get("L0_ffn_router_w"),
        "w1": get("L0_ffn_w1"),
        "b1_cols": np.ascontiguousarray(get("L0_ffn_b1").reshape(FT, P).T),
        "w2": get("L0_ffn_w2"),
        "b2_rows": np.ascontiguousarray(np.broadcast_to(get("L0_ffn_b2"), (P, D))),
        "ident": np.eye(P, dtype=np.float32),
    }
    arrays = {f"in_{k}": np.ascontiguousarray(v) for k, v in arrays.items()}
    nc = bacc.Bacc("TRN2", target_bir_lowering=False, num_devices=1)
    args = [nc.dram_tensor(k, v.shape, mybir.dt.from_np(v.dtype), kind="ExternalInput").ap()
            for k, v in arrays.items()]
    out = nc.dram_tensor("out_y", (B, SEQ, D), F32, kind="ExternalOutput").ap()
    layer_kernel(nc, *args, out)
    result = run_bass_kernel_spmd(nc, [arrays], core_ids=[0])
    return result.results[0]["out_y"]
```

```python
from contextlib import ExitStack

import concourse.bass as bass
from concourse import mybir

F32 = mybir.dt.float32
F32R = mybir.dt.float32r
ALU = mybir.AluOpType
ACT = mybir.ActivationFunctionType
AX = mybir.AxisListType

P = 128
B, SEQ, D = 8, 512, 256
HEADS, DH = 16, 64
INNER = HEADS * DH
FF = 1024
EXPERTS = 8
TT = SEQ // P
KT = D // P
FT = FF // P
PAIRS = HEADS // 2
NPAIR = B * PAIRS
NHEAD = B * HEADS
NUNIT = 2 * NHEAD
SPB = 2 * HEADS
LN_EPS = 1e-5
RMS_EPS = 1e-12
SCALE = DH ** -0.5
FIRST_SLOT = -15
LAST_SLOT = NUNIT + 3
FFN_LN_SLOT = NUNIT - 5

PS_SCORE = (0, 2)
PS_PT = 4
PS_OUT = 6
PS_AUX = 7
PS_UP = (0, 1)
PS_XT = 2
PS_ROUTER = 4
PS_LAST_OUT = 7
PS_DOWN = (5, 6)


def plan_aux():
    plan, n_blocks, index = {}, 0, {}
    for slot in range(FIRST_SLOT, LAST_SLOT + 1):
        rel = slot % SPB
        b = slot // SPB
        task = None
        if rel % 4 == 3 and 0 <= (slot + 5) // 4 < NPAIR:
            task = ("q", (slot + 5) // 4)
        elif rel % 4 == 0 and 0 <= (slot + 4) // 4 < NPAIR:
            task = ("k", (slot + 4) // 4)
        elif rel % 8 == 5 and 1 <= (slot + 3) // 8 < NPAIR // 2:
            task = ("v", (slot + 3) // 8, 0)
        elif rel % 8 == 6 and 1 <= (slot + 2) // 8 < NPAIR // 2:
            task = ("v", (slot + 2) // 8, 1)
        elif slot in (1, 2):
            task = ("v", 0, slot - 1)
        elif rel in (25, 26) and 0 <= b + 1 < B:
            task = ("xt", b + 1, rel - 25)
        elif rel in (1, 2) and 0 < b <= B:
            task = ("out", 2 * (b - 1), rel - 1)
        elif rel in (9, 10) and 0 < b < B:
            task = ("out", 2 * (b - 1) + 1, rel - 9)
        if task:
            plan[slot] = (n_blocks, *task)
            index[task] = n_blocks
            n_blocks += 1
    last = [(n_blocks + part, "out", 2 * B - 1, part) for part in range(2)]
    index.update({(kind, *args): n for n, kind, *args in last})
    return plan, index, last


def layer_kernel(nc, x, gamma_cols, w_qkv, w_out, router_w, w1, b1_cols, w2, b2_rows, ident, out):
    aux_at, aux_index, last_out = plan_aux()
    x_v = x.rearrange("b (p t) d -> b p t d", t=TT)
    out_v = out.rearrange("b (p t) d -> b p t d", t=TT)
    x1_dram = nc.dram_tensor("x1_scratch", (B, P, TT, D), F32, kind="Internal").ap()
    wqkv_v = w_qkv.rearrange("(k p) n -> p k n", p=P)
    wout_v = w_out.rearrange("(k p) n -> p k n", p=P)
    w1_v = w1.rearrange("(k p) n -> p k n", p=P)
    w2_v = w2.rearrange("(k p) n -> p k n", p=P)
    rw_v = router_w.rearrange("(k p) e -> p k e", p=P)

    with ExitStack() as ctx:
        def sb(name, shape, dt, scope=ctx):
            return scope.enter_context(nc.sbuf_tensor(name, shape, dt))

        def sem(name):
            return ctx.enter_context(nc.semaphore(name))

        ps = ctx.enter_context(nc.psum_tensor("ps", [P, 8, 512], F32))

        wbig = [sb("wbig_hi", [P, KT * 3 * INNER], F32R), sb("wbig_lo", [P, KT * 3 * INNER], F32R)]
        wqkv = [w[:, :].rearrange("p (k n) -> p k n", k=KT) for w in wbig]
        w1s = [w[:, 0:KT * FF].rearrange("p (k n) -> p k n", k=KT) for w in wbig]
        w2s = [w[:, KT * FF:KT * FF + FT * D].rearrange("p (k n) -> p k n", k=FT) for w in wbig]
        identity = sb("identity", [P, P], F32)
        gain = sb("gain", [P, KT], F32)
        gamma_sb = sb("gamma_sb", [P, KT], F32)
        b1_sb = sb("b1_sb", [P, FT], F32)
        rw_sb = sb("rw_sb", [P, KT, EXPERTS], F32)
        rw_parts = sb("rw_parts", [P, KT, 2 * EXPERTS], F32R)
        half_pos = sb("half_pos", [P, TT], F32)
        half_neg = sb("half_neg", [P, TT], F32)
        ln_stats = sb("ln_stats", [P, TT, 6], F32)
        ln_mv = sb("ln_mv", [P, TT, 2], F32)
        ln_veps = sb("ln_veps", [P, TT], F32)
        ln_std = sb("ln_std", [P, TT], F32)
        ln_rstd = sb("ln_rstd", [P, TT], F32)
        ln_norm = sb("ln_norm", [P, 3, TT], F32)
        ln_scale = sb("ln_scale", [P, TT], F32)
        wstage = sb("wstage", [P, 1024], F32)

        xbuf = sb("xbuf", [P, 2, TT, D], F32)
        xn = sb("xn", [P, TT, D], F32)
        xT = [sb("xT_hi", [P, KT, SEQ], F32R), sb("xT_lo", [P, KT, SEQ], F32R)]
        QL, QH, KH, KL = range(4)
        nat = sb("nat", [P, 4, SEQ], F32R)
        NPROB = 3
        prob = sb("prob", [P, NPROB, 1024], F32)
        pT = [sb("pT_hi", [P, 2, TT, SEQ], F32R), sb("pT_lo", [P, 2, TT, SEQ], F32R)]
        att = ctx.enter_context(ExitStack())
        NSTACK = 3
        stack = sb("stack", [P, NSTACK, 3, SEQ], F32R, att)
        vbuf = sb("vbuf", [P, 2, TT, 4, 2 * DH], F32R, att)
        wout = [sb("wout_hi", [P, PAIRS, D], F32R, att), sb("wout_lo", [P, PAIRS, D], F32R, att)]
        vlo_part = sb("vlo_part", [DH, SEQ], F32, att)
        att32 = sb("att32", [P, SEQ], F32, att)
        NATT = 7
        attT = [sb("attT_hi", [P, NATT, SEQ], F32R, att), sb("attT_lo", [P, NATT, SEQ], F32R, att)]
        negmax = sb("negmax", [P, 4, 2], F32, att)
        rowsum = sb("rowsum", [P, 4, 2], F32, att)
        rowinv = sb("rowinv", [P, 4, 2], F32, att)
        att.close()

        f_x1 = [xbuf[:, 0], prob[:, 0, :].rearrange("p (t d) -> p t d", t=TT), xbuf[:, 1]]
        f_x2 = xn
        f_xT = [(xT[0], nat[:, 0:2]), (xT[1], nat[:, 2:4])]
        f_h = [prob[:, 1, 0:SEQ], prob[:, 1, SEQ:2 * SEQ], prob[:, 2, 0:SEQ]]
        f_hT = [p[:, :, :, :].rearrange("p a k q -> p (a k) q") for p in pT]
        ffn = ctx.enter_context(ExitStack())
        b2_sb = sb("b2_sb", [P, D], F32, ffn)
        f_y = sb("f_y", [P, 2, 2, D], F32, ffn)
        f_o = sb("f_o", [P, 2, TT, D], F32, ffn)
        r_logitT = sb("r_logitT", [2 * EXPERTS, SEQ], F32, ffn)
        r_half = sb("r_half", [P, TT, EXPERTS], F32, ffn)
        r_logit = sb("r_logit", [P, TT, EXPERTS], F32, ffn)
        r_max = sb("r_max", [P, TT], F32, ffn)
        r_shift = sb("r_shift", [P, TT, EXPERTS], F32, ffn)
        r_exp = sb("r_exp", [P, TT, EXPERTS], F32, ffn)
        r_sum = sb("r_sum", [P, TT], F32, ffn)
        r_inv = sb("r_inv", [P, TT], F32, ffn)
        r_prob = sb("r_prob", [P, TT, EXPERTS], F32, ffn)
        r_top = sb("r_top", [P, TT, 8], F32, ffn)
        r_tsum = sb("r_tsum", [P, TT], F32, ffn)
        r_tinv = sb("r_tinv", [P, TT], F32, ffn)
        r_pair = sb("r_pair", [P, TT, 2], F32, ffn)
        r_weight = sb("r_weight", [P, 2, TT], F32, ffn)
        ffn.close()

        s_const = sem("const_loaded")
        s_b2 = sem("b2_loaded")
        s_x = [sem(f"x_loaded{i}") for i in range(2)]
        s_wload = [sem(f"weights_loaded{i}") for i in range(3)]
        s_wstage = sem("ffn_weights_loaded")
        s_whi = sem("weights_hi")
        s_wlo = sem("weights_lo")
        s_half = sem("exponents_set")
        s_dve = sem("dve_step")
        s_var = sem("variance_ready")
        s_pow = sem("powers_ready")
        s_xn = sem("xn_ready")
        s_score = sem("scores_done")
        s_max = sem("rowmax_done")
        s_exp = sem("exp_done")
        s_inv = sem("rowinv_done")
        s_prob = sem("probabilities_normalised")
        s_pt = sem("probabilities_transposed")
        s_pthi = sem("pT_hi_done")
        s_ptlo = sem("pT_lo_done")
        s_pv = sem("pv_done")
        s_vlo = sem("vlo_part_copied")
        s_head = sem("head_output_done")
        s_atthi = sem("attT_hi_done")
        s_att = sem("attT_done")
        s_auxfull = sem("aux_block_in_psum")
        s_auxhi = sem("aux_hi_done")
        s_aux = sem("aux_block_done")
        s_stack = [sem(f"head_stacked{i}") for i in range(NSTACK)]
        s_x1 = sem("x1_stored")
        s_fx1 = [sem(f"f_x1_loaded{i}") for i in range(3)]
        s_fx2 = sem("f_x2_ready")
        s_fxt = sem("f_x2_transposed")
        s_fxthi = sem("f_xT_hi")
        s_fxtlo = sem("f_xT_lo")
        s_frm = sem("router_product")
        s_flt = sem("router_product_copied")
        s_frt = sem("router_logits")
        s_frs = sem("router_shifted")
        s_fre = sem("router_exp")
        s_frw = sem("router_weight")
        s_up = sem("up_done")
        s_gelu = sem("gelu_done")
        s_hhi = sem("hidden_hi")
        s_hlo = sem("hidden_lo")
        s_down = sem("down_done")
        s_fy = sem("down_read")
        s_fo = sem("ffn_out_ready")
        s_out = [sem(f"out_stored{i}") for i in range(2)]

        block = ctx.enter_context(nc.Block())

        N_CONST = 5
        N_QKV_CHUNKS = 6
        N_CHUNKS = 12

        def weight_chunk(i):
            if i < 6:
                cols, k = i // 2, i % 2
                c = slice(cols * INNER, (cols + 1) * INNER)
                return wqkv_v[:, k, c], [w[:, k, c] for w in wqkv]
            if i < 8:
                c = slice((i - 6) * 4, (i - 6) * 4 + 4)
                return wout_v[:, c, :], [w[:, c, :].rearrange("p k n -> p (k n)") for w in wout]
            if i < 10:
                return w1_v[:, i - 8, :], [w[:, i - 8, :] for w in w1s]
            c = slice((i - 10) * 4, (i - 10) * 4 + 4)
            return w2_v[:, c, :], [w[:, c, :].rearrange("p k n -> p (k n)") for w in w2s]

        def weight_stage(i):
            return prob[:, i % NPROB, :] if i < N_QKV_CHUNKS else wstage[:, :]

        def wait_weight_loaded(eng, i):
            if i < N_QKV_CHUNKS:
                eng.wait_ge(s_wload[i % NPROB], 16 * (i // NPROB + 1))
            else:
                eng.wait_ge(s_wstage, 16 * (i - N_QKV_CHUNKS + 1))

        def weight_slots(slot):
            first = {-11: [0, 1], -8: [2, 3], 0: [4, 5], 10: [6], 14: [7]}
            if NUNIT - 6 <= slot < NUNIT - 2:
                return [8 + slot - (NUNIT - 6)]
            return first.get(slot, [])

        def ln_task(slot):
            if slot >= FFN_LN_SLOT:
                return (B, slot - FFN_LN_SLOT) if slot - FFN_LN_SLOT < 6 else None
            b, step = divmod(slot - 17, SPB)
            return (b + 1, step) if step < 7 and 0 <= b + 1 < B else None

        def stack_loads_before(slot_of_stack, head):
            return 48 * (head // NSTACK + 1)

        @block.sync
        def _(sp):
            sp.dma_start(xbuf[:, 0], x_v[0]).then_inc(s_x[0], 16)
            for i in range(NPROB):
                sp.dma_start(weight_stage(i), weight_chunk(i)[0]).then_inc(s_wload[i], 16)
            sp.dma_start(identity[:, :], ident).then_inc(s_const, 16)
            sp.dma_start(gamma_sb[:, :], gamma_cols).then_inc(s_const, 16)
            sp.dma_start(b1_sb[:, :], b1_cols).then_inc(s_const, 16)
            for k in range(KT):
                sp.dma_start(rw_sb[:, k, :], rw_v[:, k, :]).then_inc(s_const, 16)
            for i in range(NPROB, N_QKV_CHUNKS):
                sp.wait_ge(s_wlo, i - NPROB + 1)
                sp.dma_start(weight_stage(i), weight_chunk(i)[0]).then_inc(s_wload[i % NPROB], 16)

            for slot in range(FIRST_SLOT, LAST_SLOT + 1):
                b, rel = divmod(slot, SPB)
                if rel == 11 and 0 <= b - 1 < B:
                    sp.wait_ge(s_aux, aux_index[("out", 2 * (b - 1) + 1, 1)] + 1)
                    sp.dma_start(x1_dram[b - 1], xbuf[:, (b - 1) % 2]).then_inc(s_x1, 16)
                if rel == 12 and 1 <= b + 1 < B:
                    if b >= 1:
                        sp.wait_ge(s_x1, 16 * b)
                    sp.dma_start(xbuf[:, (b + 1) % 2], x_v[b + 1]).then_inc(s_x[(b + 1) % 2], 16)
                pair = (slot + 3) // 4
                if rel % 4 == 1 and 0 <= pair < NPAIR:
                    sp.wait_ge(s_aux, aux_index[("k", pair)] + 1)
                    for odd in range(2):
                        head = 2 * pair + odd
                        i = head % NSTACK
                        src = nat[odd * DH:(odd + 1) * DH].bitcast(F32)
                        dst = stack[:, i].bitcast(F32)
                        if head >= NSTACK:
                            sp.wait_ge(s_score, 2 * (head - NSTACK) + 2)
                        sp.dma_start(dst[0:DH, 0:3, :], src[:, QH:KL + 1, :]).then_inc(s_stack[i], 16)
                        sp.dma_start(dst[DH:P, 0:1, :], src[:, QL:QL + 1, :]).then_inc(s_stack[i], 16)
                        sp.dma_start(dst[DH:P, 1:3, :], src[:, KH:KL + 1, :]).then_inc(s_stack[i], 16)
                if slot == FFN_LN_SLOT:
                    sp.wait_ge(s_x1, 16 * (B - 1))
                    sp.dma_start(f_x1[0], x1_dram[0]).then_inc(s_fx1[0], 16)
                for i in weight_slots(slot):
                    if i >= N_QKV_CHUNKS:
                        if i > N_QKV_CHUNKS:
                            sp.wait_ge(s_wlo, i)
                        sp.dma_start(weight_stage(i), weight_chunk(i)[0]).then_inc(s_wstage, 16)

            def load_x1(c):
                sp.dma_start(f_x1[c % 3], x1_dram[c]).then_inc(s_fx1[c % 3], 16)

            def store_out(c, part):
                sp.wait_ge(s_fo, 2 * c + part + 1)
                sp.dma_start(out_v[c][:, 2 * part:2 * part + 2], f_o[:, c % 2, 2 * part:2 * part + 2])\
                    .then_inc(s_out[c % 2], 16)

            sp.wait_ge(s_pt, NUNIT)
            load_x1(1)
            sp.wait_ge(s_score, NUNIT)
            sp.dma_start(b2_sb[:, :], b2_rows).then_inc(s_b2, 16)
            sp.wait_ge(s_aux, aux_index[("out", 2 * B - 1, 1)] + 1)
            sp.dma_start(x1_dram[B - 1], xbuf[:, (B - 1) % 2]).then_inc(s_x1, 16)
            sp.wait_ge(s_x1, 16 * B)
            load_x1(2)
            for c in range(B):
                store_out(c, 0)
                store_out(c, 1)
                if c + 3 < B:
                    load_x1(c + 3)
            for i in range(2):
                sp.wait_ge(s_out[i], 32 * (B // 2))

        @block.tensor
        def _(pe):
            def products(dst, stationary, moving, first, last):
                terms = [(0, 0), (1, 0), (0, 1)]
                for n, (i, j) in enumerate(terms):
                    ins = pe.matmul(dst, stationary[i], moving[j], start=first and n == 0,
                                    stop=last and n == len(terms) - 1)
                return ins

            def scores(n):
                head, half = divmod(n, 2)
                i = head % NSTACK
                if half == 0:
                    pe.wait_ge(s_stack[i], stack_loads_before(i, head))
                if n >= 2:
                    pe.wait_ge(s_exp, n - 1)
                for j in range(2):
                    q0 = (2 * half + j) * P
                    dst = ps[:, PS_SCORE[n % 2] + j, :]
                    pe.matmul(dst, stack[:, i, 0, q0:q0 + P], stack[:, i, 1, :], start=True, stop=False)
                    ins = pe.matmul(dst, stack[:, i, 0, q0:q0 + P], stack[:, i, 2, :], start=False, stop=True)
                ins.then_inc(s_score, 1)

            def transpose_prob(n):
                pe.wait_ge(s_prob, n + 1)
                if n >= 1:
                    pe.wait_ge(s_ptlo, n)
                for j in range(2):
                    for k in range(TT):
                        ins = pe.transpose(ps[:, PS_PT + j, k * P:(k + 1) * P],
                                           prob[:, n % NPROB, j * SEQ + k * P:j * SEQ + (k + 1) * P],
                                           identity[:, :])
                ins.then_inc(s_pt, 1)

            def weighted_values(head, part):
                quad = head // 4
                if part == 0:
                    pe.wait_ge(s_ptlo, 2 * head + 2)
                    pe.wait_ge(s_aux, aux_index[("v", quad, 1)] + 1)
                    if head >= 1:
                        pe.wait_ge(s_head, head)
                for k in range(TT):
                    ins = pe.matmul(ps[:, PS_OUT, :], vbuf[:, quad % 2, k, head % 4, :],
                                    pT[part][:, head % 2, k, :], start=part == 0 and k == 0,
                                    stop=part == 1 and k == TT - 1)
                if part == 1:
                    ins.then_inc(s_pv, 1)

            def aux(block_no, kind, *args):
                if block_no >= 1:
                    pe.wait_ge(s_aux, block_no)
                bank = ps[:, PS_AUX, :]
                if kind == "xt":
                    b, k = args
                    pe.wait_ge(s_xn, b + 1)
                    if b == 0:
                        pe.wait_ge(s_const, 16 * N_CONST)
                    for t in range(TT):
                        ins = pe.transpose(bank[:, t * P:(t + 1) * P], xn[:, t, k * P:(k + 1) * P],
                                           identity[:, :])
                elif kind in "qk":
                    pair, = args
                    base = (kind == "k") * INNER + pair % PAIRS * P
                    pe.wait_ge(s_wlo, 2 if kind == "q" else 4)
                    for k in range(KT):
                        ins = products(bank, [w[:, k, base:base + P] for w in wqkv],
                                       [v[:, k, :] for v in xT], k == 0, k == KT - 1)
                elif kind == "v":
                    quad, part = args
                    base = 2 * INNER + quad % (PAIRS // 2) * 4 * DH
                    pe.wait_ge(s_wlo, 6)
                    for t in range(2):
                        c = (2 * part + t) * P
                        for k in range(KT):
                            ins = products(bank[:, t * D:(t + 1) * D], [v[:, k, c:c + P] for v in xT],
                                           [w[:, k, base:base + 4 * DH] for w in wqkv], k == 0, k == KT - 1)
                elif kind == "out":
                    half, part = args
                    pe.wait_ge(s_wlo, 8)
                    pe.wait_ge(s_att, 4 * half + 4)
                    for t in range(2):
                        c = (2 * part + t) * P
                        for j in range(4):
                            pair = 4 * half + j
                            ins = products(bank[:, t * D:(t + 1) * D],
                                           [a[:, pair % NATT, c:c + P] for a in attT],
                                           [w[:, pair % PAIRS, :] for w in wout], j == 0, j == 3)
                ins.then_inc(s_auxfull, 1)

            def transpose_x2(c):
                pe.wait_ge(s_fx2, c + 1)
                if c == 0:
                    pe.wait_ge(s_exp, NUNIT)
                else:
                    pe.wait_ge(s_fxtlo, c)
                for k in range(KT):
                    for t in range(TT):
                        ins = pe.transpose(ps[:, PS_XT + k, t * P:(t + 1) * P],
                                           f_x2[:, t, k * P:(k + 1) * P], identity[:, :])
                ins.then_inc(s_fxt, 1)

            def route(c):
                pe.wait_ge(s_fxtlo, c + 1)
                if c >= 1:
                    pe.wait_ge(s_frs, c)
                for k in range(KT):
                    for part in range(2):
                        ins = pe.matmul(ps[0:2 * EXPERTS, PS_ROUTER, :], rw_parts[:, k, :],
                                        f_xT[part][c % 2][:, k, :], start=k == 0 and part == 0,
                                        stop=k == KT - 1 and part == 1)
                ins.then_inc(s_frm, 1)

            def transpose_logits(c):
                pe.wait_ge(s_flt, c + 1)
                for t in range(TT):
                    ins = pe.transpose(ps[:, PS_ROUTER, t * 2 * EXPERTS:(t + 1) * 2 * EXPERTS],
                                       r_logitT[:, t * P:(t + 1) * P], identity[0:2 * EXPERTS, 0:2 * EXPERTS])
                ins.then_inc(s_frt, 1)

            def up(c, f):
                n = c * FT + f
                if n >= 2:
                    pe.wait_ge(s_gelu, n - 1)
                for k in range(KT):
                    ins = products(ps[:, PS_UP[n % 2], :], [w[:, k, f * P:(f + 1) * P] for w in w1s],
                                   [v[c % 2][:, k, :] for v in f_xT], k == 0, k == KT - 1)
                ins.then_inc(s_up, 1)

            def down(c, tile):
                part, t = divmod(tile, 2)
                if c >= 1 and t == 0:
                    pe.wait_ge(s_fy, 2 * (c - 1) + part + 1)
                for f in range(FT):
                    if tile == 0:
                        pe.wait_ge(s_hlo, c * FT + f + 1)
                    ins = products(ps[:, PS_DOWN[part], t * D:(t + 1) * D],
                                   [h[:, f, tile * P:(tile + 1) * P] for h in f_hT],
                                   [w[:, f, :] for w in w2s], f == 0, f == FT - 1)
                if t == 1:
                    ins.then_inc(s_down, 1)

            for slot in range(FIRST_SLOT, LAST_SLOT + 1):
                if 0 <= slot < NUNIT:
                    scores(slot)
                if slot in aux_at:
                    aux(*aux_at[slot])
                if 0 <= slot - 2 < NUNIT:
                    transpose_prob(slot - 2)
                if slot == NUNIT + 1:
                    transpose_x2(0)
                if 0 <= (slot - 4) // 2 < NHEAD:
                    weighted_values(*divmod(slot - 4, 2))

            route(0)
            pe.wait_ge(s_wlo, N_CHUNKS)
            for c in range(B):
                for f in range(FT):
                    up(c, f)
                    if c == 0 and f == 0:
                        transpose_logits(0)
                if c == 0:
                    for block_of_out in last_out:
                        aux(*block_of_out)
                if c + 1 < B:
                    transpose_x2(c + 1)
                down(c, 0)
                down(c, 1)
                if c + 1 < B:
                    route(c + 1)
                down(c, 2)
                if c + 1 < B:
                    transpose_logits(c + 1)
                down(c, 3)

        @block.scalar
        def _(act):
            def aux_hi(block_no, kind, *args):
                act.wait_ge(s_auxfull, block_no + 1)
                bank = ps[:, PS_AUX, :]
                if kind == "xt":
                    ins = act.activation(xT[0][:, args[1], :], bank, ACT.Copy, scale=gain[:, args[1]:args[1] + 1])
                elif kind == "q":
                    pair, = args
                    for head in (2 * pair - 2, 2 * pair - 1):
                        if head >= 0:
                            act.wait_ge(s_stack[head % NSTACK], stack_loads_before(head % NSTACK, head))
                    ins = act.activation(nat[:, QH, :], bank, ACT.Copy, scale=SCALE)
                elif kind == "k":
                    ins = act.activation(nat[:, KH, :], bank, ACT.Copy)
                elif kind == "v":
                    quad, part = args
                    ins = act.activation(vbuf[:, quad % 2, 2 * part:2 * part + 2, :, 0:DH],
                                         bank.rearrange("p (t h d) -> p t h d", t=2, h=4), ACT.Copy)
                ins.then_inc(s_auxhi, 1)

            def x2_hi(c):
                act.wait_ge(s_fxt, c + 1)
                act.activation(f_xT[0][c % 2][:, :, :], ps[:, PS_XT:PS_XT + 2, :], ACT.Copy).then_inc(s_fxthi, 1)

            for slot in range(FIRST_SLOT, LAST_SLOT + 1):
                if slot == NUNIT + 2:
                    x2_hi(0)
                for i in weight_slots(slot):
                    wait_weight_loaded(act, i)
                    act.activation(weight_chunk(i)[1][0], weight_stage(i), ACT.Copy).then_inc(s_whi, 1)
                if slot in aux_at and aux_at[slot][1] != "out":
                    aux_hi(*aux_at[slot])
                n = slot - 2
                if 0 <= n < NUNIT:
                    head, half = divmod(n, 2)
                    act.wait_ge(s_pt, n + 1)
                    dst = pT[0][:, head % 2, :, half * 2 * P:(half + 1) * 2 * P]
                    act.activation(dst.rearrange("p k (j q) -> p j k q", j=2),
                                   ps[:, PS_PT:PS_PT + 2, :].rearrange("p j (k q) -> p j k q", k=TT),
                                   ACT.Copy).then_inc(s_pthi, 1)
                head, part = divmod(slot - 4, 2)
                if part == 1 and 0 <= head < NHEAD:
                    act.wait_ge(s_pv, head + 1)
                    act.activation(vlo_part[:, :], ps[DH:P, PS_OUT, :], ACT.Copy).then_inc(s_vlo, 1)
                n = slot
                if 0 <= n < NUNIT:
                    act.wait_ge(s_max, n + 1)
                    if n >= NPROB:
                        act.wait_ge(s_pt, n - NPROB + 1)
                    for j in range(2):
                        ins = act.activation(prob[:, n % NPROB, j * SEQ:(j + 1) * SEQ],
                                             ps[:, PS_SCORE[n % 2] + j, :], ACT.Exp,
                                             bias=negmax[:, n % 4, j:j + 1], accum_out=rowsum[:, n % 4, j:j + 1])
                    ins.then_inc(s_exp, 1)

            def copy_logits(c):
                act.wait_ge(s_frm, c + 1)
                act.activation(r_logitT[:, :], ps[0:2 * EXPERTS, PS_ROUTER, :], ACT.Copy).then_inc(s_flt, 1)

            def router_exp(c):
                act.wait_ge(s_frs, c + 1)
                act.activation(r_exp[:, :, :], r_shift[:, :, :], ACT.Exp).then_inc(s_fre, 1)

            copy_logits(0)
            for c in range(B):
                for f in range(FT):
                    n = c * FT + f
                    act.wait_ge(s_up, n + 1)
                    if n >= 3:
                        act.wait_ge(s_hlo, n - 2)
                    act.activation(f_h[n % 3], ps[:, PS_UP[n % 2], :], ACT.Gelu_apprx_tanh,
                                   bias=b1_sb[:, f:f + 1]).then_inc(s_gelu, 1)
                if c == 0:
                    router_exp(0)
                if c + 1 < B:
                    x2_hi(c + 1)
                    copy_logits(c + 1)
                    router_exp(c + 1)

        @block.gpsimd
        def _(pool):
            pool.memset(half_pos[:, :], 0.5).then_inc(s_half, 1)
            pool.memset(half_neg[:, :], -0.5).then_inc(s_half, 1)
            pool.wait_ge(s_half, 2)

            def powers(n):
                pool.wait_ge(s_var, n + 1)
                pool.tensor_tensor(ln_std[:, :], ln_mv[:, :, 1], half_pos[:, :], ALU.pow)
                pool.tensor_tensor(ln_rstd[:, :], ln_veps[:, :], half_neg[:, :], ALU.pow).then_inc(s_pow, 1)

            def times(dst, src, scalar):
                return pool.tensor_scalar(dst, src, scalar, 1.0, ALU.mult, ALU.mult)

            for slot in range(FIRST_SLOT, LAST_SLOT + 2):
                n = slot - 1
                if 0 <= n < NUNIT:
                    pool.wait_ge(s_inv, n + 1)
                    for j in range(2):
                        p = prob[:, n % NPROB, j * SEQ:(j + 1) * SEQ]
                        ins = times(p, p, rowinv[:, n % 4, j:j + 1])
                    ins.then_inc(s_prob, 1)
                task = ln_task(slot)
                if task and task[1] == 4:
                    powers(task[0])
                pair, r = divmod(slot - 8, 4)
                if r == 0 and 0 <= pair < NPAIR:
                    pool.wait_ge(s_head, 2 * pair + 2)
                    if pair >= NATT:
                        pool.wait_ge(s_aux, aux_index[("out", (pair - NATT) // 4, 1)] + 1)
                    pool.tensor_scalar(attT[0][:, pair % NATT, :], att32[:, :], 1.0, 1.0, ALU.mult, ALU.mult)\
                        .then_inc(s_atthi, 1)
                    pool.wait_ge(s_atthi, pair + 1)
                    pool.tensor_tensor(attT[1][:, pair % NATT, :], att32[:, :], attT[0][:, pair % NATT, :],
                                       ALU.subtract).then_inc(s_att, 1)

            for c in range(B):
                for f in range(FT):
                    n = c * FT + f
                    pool.wait_ge(s_gelu, n + 1)
                    if c >= 1 and f == 0:
                        pool.wait_ge(s_down, 2 * c)
                    pool.tensor_scalar(f_hT[0][:, f, :], f_h[n % 3], 1.0, 1.0, ALU.mult, ALU.mult)\
                        .then_inc(s_hhi, 1)
                    if c == 0 and f == 4:
                        powers(B + 1)
                if c + 2 < B:
                    powers(B + c + 2)

        @block.vector
        def _(dve):
            chain = [0]

            def link(ins):
                chain[0] += 1
                ins.then_inc(s_dve, 1)
                dve.wait_ge(s_dve, chain[0])

            def statistics_step(src, t, last):
                link(dve.bn_stats(ln_stats[:, t, :], src))
                link(dve.bn_aggr(ln_mv[:, t, :], ln_stats[:, t, :]))
                if last:
                    dve.tensor_scalar(ln_veps[:, :], ln_mv[:, :, 1], LN_EPS, None, ALU.add).then_inc(s_var, 1)

            def attention_scale():
                root = float(D) ** 0.5
                link(dve.scalar_tensor_tensor(ln_norm[:, 0, :], ln_std[:, :], root, ln_rstd[:, :],
                                              ALU.mult, ALU.mult))
                link(dve.tensor_scalar(ln_norm[:, 1, :], ln_norm[:, 0, :], RMS_EPS, None, ALU.max))
                link(dve.reciprocal(ln_norm[:, 2, :], ln_norm[:, 1, :]))
                link(dve.scalar_tensor_tensor(ln_scale[:, :], ln_rstd[:, :], root, ln_norm[:, 2, :],
                                              ALU.mult, ALU.mult))

            def normalise(dst, src, t, scale):
                return dve.tensor_scalar(dst, src, ln_mv[:, t, 0:1], scale[:, t:t + 1], ALU.subtract, ALU.mult)

            def lo(dst, full, hi, scale=None):
                if scale is None:
                    return dve.tensor_tensor(dst, full, hi, ALU.subtract)
                return dve.scalar_tensor_tensor(dst, full, scale, hi, ALU.mult, ALU.subtract)

            def aux_done(block_no, kind, *args):
                bank = ps[:, PS_AUX, :]
                if kind == "out":
                    half, part = args
                    dve.wait_ge(s_auxfull, block_no + 1)
                    if half % 2 == 1:
                        dve.wait_ge(s_aux, aux_index[("out", half - 1, 1)] + 1)
                    dst = xbuf[:, half // 2 % 2, 2 * part:2 * part + 2, :].rearrange("p t d -> p (t d)")
                    dve.tensor_tensor(dst, bank, dst, ALU.add).then_inc(s_aux, 1)
                    return
                hi_no = sum(1 for k in range(block_no + 1) if aux_kind[k] != "out")
                dve.wait_ge(s_auxhi, hi_no)
                if kind == "xt":
                    k = args[1]
                    ins = lo(xT[1][:, k, :], bank, xT[0][:, k, :], gain[:, k:k + 1])
                elif kind == "q":
                    ins = lo(nat[:, QL, :], bank, nat[:, QH, :], SCALE)
                elif kind == "k":
                    ins = lo(nat[:, KL, :], bank, nat[:, KH, :])
                else:
                    quad, part = args
                    v = vbuf[:, quad % 2, 2 * part:2 * part + 2, :, :]
                    ins = lo(v[:, :, :, DH:2 * DH], bank.rearrange("p (t h d) -> p t h d", t=2, h=4),
                             v[:, :, :, 0:DH])
                ins.then_inc(s_aux, 1)

            aux_kind = [t[1] for t in sorted(aux_at.values())] + ["out"] * len(last_out)

            def ffn_stats(c, t):
                if t == 0:
                    dve.wait_ge(s_fx1[c % 3], 16 * (c // 3 + 1))
                statistics_step(f_x1[c % 3][:, t, :], t, t == TT - 1)

            def ffn_normalise(c):
                dve.wait_ge(s_pow, B + c + 1)
                if c >= 1:
                    dve.wait_ge(s_fxt, c)
                for t in range(TT):
                    ins = normalise(f_x2[:, t, :], f_x1[c % 3][:, t, :], t, ln_rstd)
                ins.then_inc(s_fx2, 1)

            def ffn_split(c):
                dve.wait_ge(s_fxthi, c + 1)
                lo(f_xT[1][c % 2][:, :, :], ps[:, PS_XT:PS_XT + 2, :], f_xT[0][c % 2][:, :, :]).then_inc(s_fxtlo, 1)

            for slot in range(FIRST_SLOT, LAST_SLOT + 1):
                n = slot
                if 0 <= n < NUNIT:
                    dve.wait_ge(s_score, n + 1)
                    dve.tensor_reduce(negmax[:, n % 4, :], ps[:, PS_SCORE[n % 2]:PS_SCORE[n % 2] + 2, :],
                                      AX.X, ALU.max, negate=True).then_inc(s_max, 1)
                n = slot - 1
                if 0 <= n < NUNIT:
                    dve.wait_ge(s_exp, n + 1)
                    dve.reciprocal(rowinv[:, n % 4, :], rowsum[:, n % 4, :]).then_inc(s_inv, 1)
                if slot in aux_at:
                    aux_done(*aux_at[slot])
                n = slot - 2
                if 0 <= n < NUNIT:
                    head, half = divmod(n, 2)
                    dve.wait_ge(s_pthi, n + 1)
                    part = [p[:, head % 2, :, half * 2 * P:(half + 1) * 2 * P].rearrange(
                        "p k (j q) -> p j k q", j=2) for p in pT]
                    lo(part[1], ps[:, PS_PT:PS_PT + 2, :].rearrange("p j (k q) -> p j k q", k=TT),
                       part[0]).then_inc(s_ptlo, 1)
                if slot == NUNIT + 2:
                    ffn_split(0)
                head, part = divmod(slot - 4, 2)
                if part == 1 and 0 <= head < NHEAD:
                    dve.wait_ge(s_vlo, head + 1)
                    if head >= 2 and head % 2 == 0:
                        dve.wait_ge(s_att, head // 2)
                    dve.tensor_tensor(att32[head % 2 * DH:(head % 2 + 1) * DH, :], ps[0:DH, PS_OUT, :],
                                      vlo_part[:, :], ALU.add).then_inc(s_head, 1)
                for i in weight_slots(slot):
                    if i == 0:
                        dve.wait_ge(s_const, 16 * N_CONST)
                        dve.tensor_scalar(gain[:, :], gamma_sb[:, :], 1.0, None, ALU.add)
                        link(dve.tensor_copy(rw_parts[:, :, 0:EXPERTS], rw_sb[:, :, :]))
                        link(lo(rw_parts[:, :, EXPERTS:], rw_sb[:, :, :], rw_parts[:, :, 0:EXPERTS]))
                    dve.wait_ge(s_whi, i + 1)
                    hi_part, lo_part = weight_chunk(i)[1]
                    lo(lo_part, weight_stage(i), hi_part).then_inc(s_wlo, 1)
                task = ln_task(slot)
                if task:
                    b, step = task
                    xb = xbuf[:, b % 2]
                    if step == 0 and b == B:
                        dve.wait_ge(s_fx1[0], 16)
                    elif step == 0:
                        dve.wait_ge(s_x[b % 2], 16 * (b // 2 + 1))
                    if step < 4:
                        statistics_step(xb[:, step, :], step, step == 3)
                    elif step == 5 and b == B:
                        ffn_normalise(0)
                    elif step == 5:
                        dve.wait_ge(s_pow, b + 1)
                        attention_scale()
                    elif step == 6:
                        for t in range(TT):
                            ins = normalise(xn[:, t, :], xb[:, t, :], t, ln_scale)
                        ins.then_inc(s_xn, 1)

            def routing_shift(c):
                dve.wait_ge(s_frt, c + 1)
                logits = ps[:, PS_ROUTER, 0:TT * 2 * EXPERTS].rearrange("p (t e) -> p t e", t=TT)
                link(dve.tensor_copy(r_half[:, :, :], logits[:, :, EXPERTS:]))
                link(dve.tensor_tensor(r_logit[:, :, :], logits[:, :, 0:EXPERTS], r_half[:, :, :], ALU.add))
                link(dve.tensor_reduce(r_max[:, :], r_logit[:, :, :], AX.X, ALU.max))
                dve.tensor_tensor(r_shift[:, :, :], r_logit[:, :, :],
                                  r_max[:, :].unsqueeze(2).broadcast_to((P, TT, EXPERTS)),
                                  ALU.subtract).then_inc(s_frs, 1)

            def routing_weight(c):
                dve.wait_ge(s_fre, c + 1)
                link(dve.reduce_sum(r_sum[:, :], r_exp[:, :, :], AX.X))
                link(dve.reciprocal(r_inv[:, :], r_sum[:, :]))
                link(dve.tensor_tensor(r_prob[:, :, :], r_exp[:, :, :],
                                       r_inv[:, :].unsqueeze(2).broadcast_to((P, TT, EXPERTS)), ALU.mult))
                for t in range(TT):
                    ins = dve.max(r_top[:, t, :], r_prob[:, t, :])
                link(ins)
                link(dve.tensor_tensor(r_tsum[:, :], r_top[:, :, 0], r_top[:, :, 1], ALU.add))
                link(dve.reciprocal(r_tinv[:, :], r_tsum[:, :]))
                link(dve.tensor_tensor(r_pair[:, :, :], r_top[:, :, 0:2],
                                       r_tinv[:, :].unsqueeze(2).broadcast_to((P, TT, 2)), ALU.mult))
                link(dve.tensor_tensor(r_weight[:, c % 2, :], r_pair[:, :, 0], r_pair[:, :, 1], ALU.add))

            def finish(c, part):
                if c == 0 and part == 0:
                    dve.wait_ge(s_b2, 16)
                dve.wait_ge(s_down, 2 * c + part + 1)
                if part == 0 and c >= 2:
                    dve.wait_ge(s_out[c % 2], 32 * (c // 2))
                y = f_y[:, part]
                dve.tensor_tensor(y, ps[:, PS_DOWN[part], :].rearrange("p (t d) -> p t d", t=2),
                                  b2_sb[:, :].unsqueeze(1).broadcast_to((P, 2, D)), ALU.add).then_inc(s_fy, 1)
                dve.wait_ge(s_fy, 2 * c + part + 1)
                for t in range(2):
                    tile = 2 * part + t
                    ins = dve.scalar_tensor_tensor(f_o[:, c % 2, tile, :], y[:, t, :],
                                                   r_weight[:, c % 2, tile:tile + 1],
                                                   f_x1[c % 3][:, tile, :], ALU.mult, ALU.add)
                ins.then_inc(s_fo, 1)

            for c in range(B):
                for f in range(FT):
                    n = c * FT + f
                    dve.wait_ge(s_hhi, n + 1)
                    lo(f_hT[1][:, f, :], f_h[n % 3], f_hT[0][:, f, :]).then_inc(s_hlo, 1)
                    if c == 0 and f == 0:
                        routing_shift(0)
                    if c == 0 and 1 <= f <= TT:
                        ffn_stats(1, f - 1)
                    if c == 0 and f == 6:
                        ffn_normalise(1)
                if c == 0:
                    for block_of_out in last_out:
                        aux_done(*block_of_out)
                    routing_weight(0)
                if c + 1 < B:
                    ffn_split(c + 1)
                if c + 2 < B:
                    for t in range(TT):
                        ffn_stats(c + 2, t)
                    ffn_normalise(c + 2)
                finish(c, 0)
                if c + 1 < B:
                    routing_shift(c + 1)
                    routing_weight(c + 1)
                finish(c, 1)


def kernel(**inputs):
    import numpy as np
    import concourse.bacc as bacc
    from concourse.bass_utils import run_bass_kernel_spmd

    get = lambda name: np.asarray(inputs[name])
    arrays = {
        "x": get("L0_attn_x"),
        "gamma_cols": np.ascontiguousarray(get("L0_attn_gamma").reshape(KT, P).T),
        "w_qkv": get("L0_attn_w_qkv"),
        "w_out": get("L0_attn_w_out"),
        "router_w": get("L0_ffn_router_w"),
        "w1": get("L0_ffn_w1"),
        "b1_cols": np.ascontiguousarray(get("L0_ffn_b1").reshape(FT, P).T),
        "w2": get("L0_ffn_w2"),
        "b2_rows": np.ascontiguousarray(np.broadcast_to(get("L0_ffn_b2"), (P, D))),
        "ident": np.eye(P, dtype=np.float32),
    }
    arrays = {f"in_{k}": np.ascontiguousarray(v) for k, v in arrays.items()}
    nc = bacc.Bacc("TRN2", target_bir_lowering=False, num_devices=1)
    args = [nc.dram_tensor(k, v.shape, mybir.dt.from_np(v.dtype), kind="ExternalInput").ap()
            for k, v in arrays.items()]
    out = nc.dram_tensor("out_y", (B, SEQ, D), F32, kind="ExternalOutput").ap()
    layer_kernel(nc, *args, out)
    result = run_bass_kernel_spmd(nc, [arrays], core_ids=[0])
    return result.results[0]["out_y"]
```

```python
from contextlib import ExitStack

import concourse.bass as bass
from concourse import mybir

F32 = mybir.dt.float32
F32R = mybir.dt.float32r
ALU = mybir.AluOpType
ACT = mybir.ActivationFunctionType
AX = mybir.AxisListType

P = 128
B, SEQ, D = 8, 512, 256
HEADS, DH = 16, 64
INNER = HEADS * DH
FF = 1024
EXPERTS = 8
TT = SEQ // P
KT = D // P
FT = FF // P
PAIRS = HEADS // 2
NPAIR = B * PAIRS
NHEAD = B * HEADS
NUNIT = 2 * NHEAD
SPB = 2 * HEADS
LN_EPS = 1e-5
RMS_EPS = 1e-12
SCALE = DH ** -0.5
LN_SLOT = 13
FIRST_SLOT = LN_SLOT - SPB
LAST_SLOT = NUNIT + 3
UP_SLOT = NUNIT
TAIL_UPS = 4

PS_SCORE = (0, 2)
PS_PT = 4
PS_OUT = 6
PS_AUX = 7
PS_UP = (0, 1)
PS_XT = 2
PS_ROUTER = 4
PS_DOWN = (5, 6)
PS_LAST_OUT = (7, 6, 5, 4)
PS_EARLY = (7, 6, 4, 5, 7, 6, 7)


def plan_aux():
    plan, index = {}, {}

    def add(slot, *task):
        index[task] = len(index)
        plan.setdefault(slot, []).append((index[task], *task))

    for slot in range(FIRST_SLOT, LAST_SLOT + 1):
        b, rel = divmod(slot, SPB)
        q_pair, k_pair = (slot + 5) // 4, (slot + 4) // 4
        if rel % 4 == 3 and q_pair in range(NPAIR) and q_pair != 1:
            add(slot, "q", q_pair)
        if rel % 4 == 0 and k_pair in range(NPAIR) and k_pair != 1:
            add(slot, "k", k_pair)
        if slot == 1:
            add(slot, "q", 1)
            add(slot, "k", 1)
        if rel % 8 in (5, 6) and (slot + 3) // 8 in range(1, NPAIR // 2):
            add(slot, "v", (slot + 3) // 8, rel % 8 - 5)
        if slot in (-3, 2):
            add(slot, "v", 0, int(slot > 0))
        if rel in (25, 26) and 0 <= b + 1 <= B:
            add(slot, "xt", b + 1, rel - 25)
        if rel in (25, 26) and 0 <= b < B - 1:
            add(slot, "out", 2 * b, rel - 25)
        if rel in (28, 29, 30, 31) and b == B - 1:
            add(slot, "out", 2 * b, rel - 28)
        if rel in (1, 2) and 0 < b < B:
            add(slot, "out", 2 * (b - 1), rel + 1)
        if rel in (9, 10, 17, 18) and 0 < b < B:
            add(slot, "out", 2 * (b - 1) + 1, (9, 10, 17, 18).index(rel))
    for tile in range(TT):
        add(LAST_SLOT + 1, "out", 2 * B - 1, tile)
    return plan, index, plan.pop(LAST_SLOT + 1)


def layer_kernel(nc, x, gamma_cols, w_qkv, w_out, router_w, w1, b1_cols, w2, b2_rows, ident, out):
    aux_at, aux_index, last_out = plan_aux()
    x_v = x.rearrange("b (p t) d -> b p t d", t=TT)
    out_v = out.rearrange("b (p t) d -> b p t d", t=TT)
    x1_dram = nc.dram_tensor("x1_scratch", (B, P, TT, D), F32, kind="Internal").ap()
    wqkv_v = w_qkv.rearrange("(k p) n -> p k n", p=P)
    wout_v = w_out.rearrange("(k p) n -> p k n", p=P)
    w1_v = w1.rearrange("(k p) n -> p k n", p=P)
    w2_v = w2.rearrange("(k p) n -> p k n", p=P)
    rw_v = router_w.rearrange("(k p) e -> p k e", p=P)

    with ExitStack() as ctx:
        def sb(name, shape, dt, scope=ctx):
            return scope.enter_context(nc.sbuf_tensor(name, shape, dt))

        def sem(name):
            return ctx.enter_context(nc.semaphore(name))

        ps = ctx.enter_context(nc.psum_tensor("ps", [P, 8, 512], F32))

        wbig = [sb("wbig_hi", [P, KT * 3 * INNER], F32R), sb("wbig_lo", [P, KT * 3 * INNER], F32R)]
        wqkv = [w[:, :].rearrange("p (k n) -> p k n", k=KT) for w in wbig]
        w1s = [w[:, 0:KT * FF].rearrange("p (k n) -> p k n", k=KT) for w in wbig]
        w2s = [w[:, KT * FF:KT * FF + FT * D].rearrange("p (k n) -> p k n", k=FT) for w in wbig]
        identity = sb("identity", [P, P], F32)
        gain = sb("gain", [P, KT], F32)
        gamma_sb = sb("gamma_sb", [P, KT], F32)
        b1_sb = sb("b1_sb", [P, FT], F32)
        rw_sb = sb("rw_sb", [P, KT, EXPERTS], F32)
        rw_parts = sb("rw_parts", [P, KT, 2 * EXPERTS], F32R)
        halves = sb("halves", [P, 2, TT], F32)
        ln_stats = sb("ln_stats", [P, TT, 6], F32)
        ln_mv = sb("ln_mv", [P, TT, 2], F32)
        ln_var = sb("ln_var", [P, 2, TT], F32)
        ln_pow = sb("ln_pow", [P, 2, TT], F32)
        ln_std, ln_rstd = ln_pow[:, 0, :], ln_pow[:, 1, :]
        ln_norm = sb("ln_norm", [P, 3, TT], F32)
        ln_scale = sb("ln_scale", [P, TT], F32)
        wstage = sb("wstage", [P, 1024], F32)

        xin = sb("xin", [P, TT, D], F32)
        xres = sb("xres", [P, TT, D], F32)
        xn = sb("xn", [P, TT, D], F32)
        xT = [sb("xT_hi", [P, KT, SEQ], F32R), sb("xT_lo", [P, KT, SEQ], F32R)]
        QL, QH, KH, KL = range(4)
        nat = sb("nat", [P, 4, SEQ], F32R)
        NPROB = 3
        prob = sb("prob", [P, NPROB, 1024], F32)
        pT = [sb("pT_hi", [P, 2, TT, SEQ], F32R), sb("pT_lo", [P, 2, TT, SEQ], F32R)]
        att = ctx.enter_context(ExitStack())
        NSTACK = 3
        stack = sb("stack", [P, NSTACK, 3, SEQ], F32R, att)
        vbuf = sb("vbuf", [P, 2, TT, 4, 2 * DH], F32R, att)
        wout = [sb("wout_hi", [P, PAIRS, D], F32R, att), sb("wout_lo", [P, PAIRS, D], F32R, att)]
        vlo_part = sb("vlo_part", [DH, SEQ], F32, att)
        att32 = sb("att32", [P, SEQ], F32, att)
        NATT = 7
        attT = [sb("attT_hi", [P, NATT, SEQ], F32R, att), sb("attT_lo", [P, NATT, SEQ], F32R, att)]
        negmax = sb("negmax", [P, 4, 2], F32, att)
        rowsum = sb("rowsum", [P, 4, 2], F32, att)
        rowinv = sb("rowinv", [P, 4, 2], F32, att)
        att.close()

        f_x1 = [xin[:, :, :], prob[:, 0, :].rearrange("p (t d) -> p t d", t=TT), xres[:, :, :]]
        f_x2 = xn
        f_xT = [(xT[0], nat[:, 0:2]), (xT[1], nat[:, 2:4])]
        f_h = [prob[:, 1, 0:SEQ], prob[:, 1, SEQ:2 * SEQ], prob[:, 2, 0:SEQ]]
        f_hT = [p[:, :, :, :].rearrange("p a k q -> p (a k) q") for p in pT]
        ffn = ctx.enter_context(ExitStack())
        b2_sb = sb("b2_sb", [P, D], F32, ffn)
        f_y = sb("f_y", [P, 2, 2, D], F32, ffn)
        f_o = sb("f_o", [P, 2, TT, D], F32, ffn)
        r_logitT = sb("r_logitT", [2 * EXPERTS, SEQ], F32, ffn)
        r_half = sb("r_half", [P, TT, EXPERTS], F32, ffn)
        r_logit = sb("r_logit", [P, TT, EXPERTS], F32, ffn)
        r_max = sb("r_max", [P, TT], F32, ffn)
        r_shift = sb("r_shift", [P, TT, EXPERTS], F32, ffn)
        r_exp = sb("r_exp", [P, TT, EXPERTS], F32, ffn)
        r_sum = sb("r_sum", [P, TT], F32, ffn)
        r_inv = sb("r_inv", [P, TT], F32, ffn)
        r_prob = sb("r_prob", [P, TT, EXPERTS], F32, ffn)
        r_top = sb("r_top", [P, TT, 8], F32, ffn)
        r_tsum = sb("r_tsum", [P, TT], F32, ffn)
        r_tinv = sb("r_tinv", [P, TT], F32, ffn)
        r_pair = sb("r_pair", [P, TT, 2], F32, ffn)
        r_weight = sb("r_weight", [P, 2, TT], F32, ffn)
        ffn.close()

        s_const = sem("const_loaded")
        s_router = sem("router_weights_loaded")
        s_b2 = sem("b2_loaded")
        s_x = sem("x_loaded")
        s_xres = sem("residual_loaded")
        s_wload = [sem(f"weights_loaded{i}") for i in range(4)]
        s_whi = sem("weights_hi")
        s_wlo = sem("weights_lo")
        s_wlo_pool = sem("weights_lo_pool")
        s_half = sem("exponents_set")
        s_dve = sem("dve_step")
        s_var = sem("variance_ready")
        s_pow = sem("powers_ready")
        s_xn = sem("xn_ready")
        s_score = sem("scores_done")
        s_max = sem("rowmax_done")
        s_exp = sem("exp_done")
        s_inv = sem("rowinv_done")
        s_prob = sem("probabilities_normalised")
        s_pt = sem("probabilities_transposed")
        s_pthi = sem("pT_hi_done")
        s_ptlo = sem("pT_lo_done")
        s_pv = sem("pv_done")
        s_vlo = sem("vlo_part_copied")
        s_head = sem("head_output_done")
        s_atthi = sem("attT_hi_done")
        s_att = sem("attT_done")
        s_auxfull = sem("aux_block_in_psum")
        s_auxhi = sem("aux_hi_done")
        s_aux = sem("aux_block_done")
        s_stack = [sem(f"head_stacked{i}") for i in range(NSTACK)]
        s_x1 = sem("x1_stored")
        s_fx1 = [sem(f"f_x1_loaded{i}") for i in range(3)]
        s_fx2 = sem("f_x2_ready")
        s_fxt = sem("f_x2_transposed")
        s_fxthi = sem("f_xT_hi")
        s_fxtlo = sem("f_xT_lo")
        s_frm = sem("router_product")
        s_flt = sem("router_product_copied")
        s_frt = sem("router_logits")
        s_frs = sem("router_shifted")
        s_fre = sem("router_exp")
        s_up = sem("up_done")
        s_gelu = sem("gelu_done")
        s_hhi = sem("hidden_hi")
        s_hlo = sem("hidden_lo")
        s_down = sem("down_done")
        s_fy = sem("down_read")
        s_fo = sem("ffn_out_ready")
        s_out = [sem(f"out_stored{i}") for i in range(2)]

        block = ctx.enter_context(nc.Block())

        def aux_bank(block_no):
            last = block_no - last_out[0][0]
            if last >= 0:
                return PS_LAST_OUT[last]
            return PS_EARLY[block_no] if block_no < len(PS_EARLY) else PS_AUX

        N_CONST = 2
        N_CHUNKS = 12

        def weight_chunk(i):
            if i < 6:
                cols, k = i // 2, i % 2
                c = slice(cols * INNER, (cols + 1) * INNER)
                return wqkv_v[:, k, c], [w[:, k, c] for w in wqkv]
            if i < 8:
                c = slice((i - 6) * 4, (i - 6) * 4 + 4)
                return wout_v[:, c, :], [w[:, c, :].rearrange("p k n -> p (k n)") for w in wout]
            if i < 10:
                return w1_v[:, i - 8, :], [w[:, i - 8, :] for w in w1s]
            c = slice((i - 10) * 4, (i - 10) * 4 + 4)
            return w2_v[:, c, :], [w[:, c, :].rearrange("p k n -> p (k n)") for w in w2s]

        stage_of = [0, 1, 2, 3, 0, 1] + [3] * (N_CHUNKS - 6)
        nth_in_stage = [stage_of[:i].count(stage_of[i]) for i in range(N_CHUNKS)]
        POOL_CHUNKS = (2, 3, 8, 9, 10, 11)
        slot_of_chunks = {FIRST_SLOT + 4: [0], FIRST_SLOT + 9: [1], -8: [2, 3], -6: [4, 5], 6: [6], 10: [7]}
        slot_of_chunks.update({NUNIT - 6: [8], NUNIT - 4: [9], NUNIT - 2: [10], NUNIT + 2: [11]})

        HIDDEN_SLOTS = [UP_SLOT + 2, UP_SLOT + 3]

        def weight_stage(i):
            return prob[:, stage_of[i], :] if stage_of[i] < NPROB else wstage[:, :]

        def wait_weight_loaded(eng, i):
            eng.wait_ge(s_wload[stage_of[i]], 16 * (nth_in_stage[i] + 1))

        def wait_weight_split(eng, i):
            if i in POOL_CHUNKS:
                eng.wait_ge(s_wlo_pool, POOL_CHUNKS.index(i) + 1)
            else:
                eng.wait_ge(s_wlo, i + 1 - sum(j < i for j in POOL_CHUNKS))

        def load_weight(sp, i):
            if nth_in_stage[i]:
                wait_weight_split(sp, max(j for j in range(i) if stage_of[j] == stage_of[i]))
            sp.dma_start(weight_stage(i), weight_chunk(i)[0]).then_inc(s_wload[stage_of[i]], 16)

        def weight_slots(slot):
            return slot_of_chunks.get(slot, [])

        def ln_task(slot):
            b, step = divmod(slot - LN_SLOT, SPB)
            return (b + 1, step) if step < 9 and 0 <= b + 1 <= B else None

        def aux_of(slot):
            blocks = aux_at.get(slot, [])
            cut = len(blocks) if slot < 0 else 1
            return blocks[:cut], blocks[cut:]

        def stack_count(head):
            return 48 * (head // NSTACK + (head % NSTACK > 0))

        @block.sync
        def _(sp):
            sp.dma_start(xin[:, :, :], x_v[0]).then_inc(s_x, 16)
            load_weight(sp, 0)
            sp.dma_start(identity[:, :], ident).then_inc(s_const, 16)
            sp.dma_start(gamma_sb[:, :], gamma_cols).then_inc(s_const, 16)
            for i in range(1, 7):
                load_weight(sp, i)
            sp.dma_start(b1_sb[:, :], b1_cols).then_inc(s_router, 16)
            for k in range(KT):
                sp.dma_start(rw_sb[:, k, :], rw_v[:, k, :]).then_inc(s_router, 16)

            for slot in range(FIRST_SLOT, LAST_SLOT + 1):
                b, rel = divmod(slot, SPB)
                if rel == 24 and b + 2 < B:
                    sp.wait_ge(s_xn, b + 2)
                    sp.dma_start(xin[:, :, :], x_v[b + 2]).then_inc(s_x, 16)
                if rel == 24 and b + 2 == B:
                    sp.wait_ge(s_xn, B)
                    sp.wait_ge(s_x1, 16)
                    sp.dma_start(f_x1[0], x1_dram[0]).then_inc(s_fx1[0], 16)
                if rel == 19 and 1 <= b < B:
                    sp.wait_ge(s_aux, aux_index[("out", 2 * b - 1, TT - 1)] + 1)
                    sp.dma_start(x1_dram[b - 1], xres[:, :, :]).then_inc(s_x1, 16)
                if rel == 20 and 0 <= b < B:
                    if b >= 1:
                        sp.wait_ge(s_x1, 16 * b)
                    sp.dma_start(xres[:, :, :], x_v[b]).then_inc(s_xres, 16)
                pair = (slot + 3) // 4
                if rel % 4 == 1 and 0 <= pair < NPAIR:
                    sp.wait_ge(s_aux, aux_index[("k", pair)] + 1)
                    for odd in range(pair == 0, 2):
                        head = 2 * pair + odd
                        i = head % NSTACK
                        src = nat[odd * DH:(odd + 1) * DH].bitcast(F32)
                        dst = stack[:, i].bitcast(F32)
                        if head > NSTACK:
                            sp.wait_ge(s_score, 2 * (head - NSTACK) + 2)
                        sp.dma_start(dst[0:DH, 0:3, :], src[:, QH:KL + 1, :]).then_inc(s_stack[i], 16)
                        sp.dma_start(dst[DH:P, 0:1, :], src[:, QL:QL + 1, :]).then_inc(s_stack[i], 16)
                        sp.dma_start(dst[DH:P, 1:3, :], src[:, KH:KL + 1, :]).then_inc(s_stack[i], 16)
                for i in weight_slots(slot - 1):
                    if 6 < i + 1 < N_CHUNKS:
                        load_weight(sp, i + 1)

            def load_x1(c):
                sp.dma_start(f_x1[c % 3], x1_dram[c]).then_inc(s_fx1[c % 3], 16)

            def store_out(c, part):
                sp.wait_ge(s_fo, 2 * c + part + 1)
                sp.dma_start(out_v[c][:, 2 * part:2 * part + 2], f_o[:, c % 2, 2 * part:2 * part + 2])\
                    .then_inc(s_out[c % 2], 16)

            sp.wait_ge(s_pt, 2 * NUNIT)
            load_x1(1)
            sp.wait_ge(s_score, NUNIT)
            sp.dma_start(b2_sb[:, :], b2_rows).then_inc(s_b2, 16)
            sp.wait_ge(s_aux, aux_index[("out", 2 * B - 1, TT - 1)] + 1)
            sp.dma_start(x1_dram[B - 1], xres[:, :, :]).then_inc(s_x1, 16)
            sp.wait_ge(s_x1, 16 * B)
            load_x1(2)
            for c in range(B):
                store_out(c, 0)
                store_out(c, 1)
                if c + 3 < B:
                    load_x1(c + 3)
            for i in range(2):
                sp.wait_ge(s_out[i], 32 * (B // 2))

        @block.tensor
        def _(pe):
            def products(dst, stationary, moving, first, last):
                terms = [(0, 0), (1, 0), (0, 1)]
                for n, (i, j) in enumerate(terms):
                    ins = pe.matmul(dst, stationary[i], moving[j], start=first and n == 0,
                                    stop=last and n == len(terms) - 1)
                return ins

            def scores(n):
                head, half = divmod(n, 2)
                i = head % NSTACK
                if head == 0:
                    if half == 0:
                        pe.wait_ge(s_aux, aux_index[("k", 0)] + 1)
                elif half == 0:
                    pe.wait_ge(s_stack[i], stack_count(head))
                for j in range(2):
                    if n >= 2:
                        pe.wait_ge(s_exp, 2 * (n - 2) + j + 1)
                    q0 = (2 * half + j) * P
                    dst = ps[:, PS_SCORE[n % 2] + j, :]
                    if head == 0:
                        ins = products(dst, [nat[0:DH, part, q0:q0 + P] for part in (QH, QL)],
                                       [nat[0:DH, part, :] for part in (KH, KL)], True, True)
                        continue
                    pe.matmul(dst, stack[:, i, 0, q0:q0 + P], stack[:, i, 1, :], start=True, stop=False)
                    ins = pe.matmul(dst, stack[:, i, 0, q0:q0 + P], stack[:, i, 2, :], start=False, stop=True)
                ins.then_inc(s_score, 1)

            def transpose_prob(n):
                for j in range(2):
                    pe.wait_ge(s_prob, 2 * n + j + 1)
                    if n >= 1:
                        pe.wait_ge(s_ptlo, 2 * n - 1 + j)
                    for k in range(TT):
                        ins = pe.transpose(ps[:, PS_PT + j, k * P:(k + 1) * P],
                                           prob[:, n % NPROB, j * SEQ + k * P:j * SEQ + (k + 1) * P],
                                           identity[:, :])
                    ins.then_inc(s_pt, 1)

            def weighted_values(head, part):
                quad = head // 4
                if part == 0:
                    pe.wait_ge(s_ptlo, 4 * head + 4)
                    pe.wait_ge(s_aux, aux_index[("v", quad, 1)] + 1)
                    if head >= 1:
                        pe.wait_ge(s_head, head)
                for k in range(TT):
                    ins = pe.matmul(ps[:, PS_OUT, :], vbuf[:, quad % 2, k, head % 4, :],
                                    pT[part][:, head % 2, k, :], start=part == 0 and k == 0,
                                    stop=part == 1 and k == TT - 1)
                if part == 1:
                    ins.then_inc(s_pv, 1)

            def aux(block_no, kind, *args):
                same_bank = [j + 1 for j in range(block_no) if aux_bank(j) == aux_bank(block_no)]
                done = max(same_bank[-1:] + [2 if block_no >= 2 else 0])
                if done:
                    pe.wait_ge(s_aux, done)
                bank = ps[:, aux_bank(block_no), :]
                if kind == "xt":
                    b, k = args
                    if b < B:
                        pe.wait_ge(s_xn, b + 1)
                    else:
                        pe.wait_ge(s_fx2, 1)
                    if b == 0:
                        pe.wait_ge(s_const, 16 * N_CONST)
                    for t in range(TT):
                        ins = pe.transpose(bank[:, t * P:(t + 1) * P], xn[:, t, k * P:(k + 1) * P],
                                           identity[:, :])
                elif kind in "qk":
                    pair, = args
                    base = (kind == "k") * INNER + pair % PAIRS * P
                    wait_weight_split(pe, 1 if kind == "q" else 3)
                    if kind == "k":
                        pe.wait_ge(s_whi, 4)
                    for k in range(KT):
                        ins = products(bank, [w[:, k, base:base + P] for w in wqkv],
                                       [v[:, k, :] for v in xT], k == 0, k == KT - 1)
                elif kind == "v":
                    quad, part = args
                    base = 2 * INNER + quad % (PAIRS // 2) * 4 * DH
                    wait_weight_split(pe, 5)
                    for t in range(2):
                        c = (2 * part + t) * P
                        for k in range(KT):
                            ins = products(bank[:, t * D:(t + 1) * D], [v[:, k, c:c + P] for v in xT],
                                           [w[:, k, base:base + 4 * DH] for w in wqkv], k == 0, k == KT - 1)
                elif kind == "out":
                    half, tile = args
                    wait_weight_split(pe, 7)
                    for j in range(4):
                        pair = 4 * half + j
                        if tile == 0:
                            pe.wait_ge(s_att, pair + 1)
                        ins = products(bank[:, 0:D],
                                       [a[:, pair % NATT, tile * P:(tile + 1) * P] for a in attT],
                                       [w[:, pair % PAIRS, :] for w in wout], j == 0, j == 3)
                ins.then_inc(s_auxfull, 1)

            def wait_x2_split(c):
                if c == 0:
                    pe.wait_ge(s_aux, aux_index[("xt", B, KT - 1)] + 1)
                else:
                    pe.wait_ge(s_fxtlo, c)

            def transpose_x2(c):
                pe.wait_ge(s_fx2, c + 1)
                if c >= 2:
                    pe.wait_ge(s_fxtlo, c - 1)
                for k in range(KT):
                    for t in range(TT):
                        ins = pe.transpose(ps[:, PS_XT + k, t * P:(t + 1) * P],
                                           f_x2[:, t, k * P:(k + 1) * P], identity[:, :])
                ins.then_inc(s_fxt, 1)

            def route(c):
                wait_x2_split(c)
                if c >= 1:
                    pe.wait_ge(s_frs, c)
                for k in range(KT):
                    for part in range(2):
                        ins = pe.matmul(ps[0:2 * EXPERTS, PS_ROUTER, :], rw_parts[:, k, :],
                                        f_xT[part][c % 2][:, k, :], start=k == 0 and part == 0,
                                        stop=k == KT - 1 and part == 1)
                ins.then_inc(s_frm, 1)

            def transpose_logits(c):
                pe.wait_ge(s_flt, c + 1)
                for t in range(TT):
                    ins = pe.transpose(ps[:, PS_ROUTER, t * 2 * EXPERTS:(t + 1) * 2 * EXPERTS],
                                       r_logitT[:, t * P:(t + 1) * P], identity[0:2 * EXPERTS, 0:2 * EXPERTS])
                ins.then_inc(s_frt, 1)

            def up(c, f):
                n = c * FT + f
                if n == 0:
                    wait_x2_split(0)
                    wait_weight_split(pe, 9)
                    pe.wait_ge(s_exp, 2 * NUNIT - 2)
                if n >= 2:
                    pe.wait_ge(s_gelu, n - 1)
                for k in range(KT):
                    ins = products(ps[:, PS_UP[n % 2], :], [w[:, k, f * P:(f + 1) * P] for w in w1s],
                                   [v[c % 2][:, k, :] for v in f_xT], k == 0, k == KT - 1)
                ins.then_inc(s_up, 1)

            def down(c, tile):
                part, t = divmod(tile, 2)
                if c >= 1 and t == 0:
                    pe.wait_ge(s_fy, 2 * (c - 1) + part + 1)
                for f in range(FT):
                    if tile == 0:
                        pe.wait_ge(s_hlo, c * FT + f + 1)
                    ins = products(ps[:, PS_DOWN[part], t * D:(t + 1) * D],
                                   [h[:, f, tile * P:(tile + 1) * P] for h in f_hT],
                                   [w[:, f, :] for w in w2s], f == 0, f == FT - 1)
                if t == 1:
                    ins.then_inc(s_down, 1)

            for slot in range(FIRST_SLOT, LAST_SLOT + 1):
                if 0 <= slot < NUNIT:
                    scores(slot)
                early, late = aux_of(slot)
                for block_of_aux in early:
                    aux(*block_of_aux)
                if 0 <= slot - UP_SLOT < TAIL_UPS:
                    up(0, slot - UP_SLOT)
                if 0 <= slot - 2 < NUNIT:
                    transpose_prob(slot - 2)
                if 0 <= (slot - 4) // 2 < NHEAD:
                    weighted_values(*divmod(slot - 4, 2))
                for block_of_aux in late:
                    aux(*block_of_aux)

            route(0)
            for c in range(B):
                for f in range(TAIL_UPS if c == 0 else 0, FT):
                    up(c, f)
                    if c == 0 and f == TAIL_UPS:
                        transpose_logits(0)
                if c == 0:
                    for block_of_out in last_out:
                        if block_of_out == last_out[-1]:
                            pe.wait_ge(s_frs, 1)
                        aux(*block_of_out)
                    wait_weight_split(pe, N_CHUNKS - 1)
                if c + 1 < B:
                    transpose_x2(c + 1)
                if c == 0:
                    pe.wait_ge(s_aux, len(aux_index))
                down(c, 0)
                down(c, 1)
                if c + 1 < B:
                    route(c + 1)
                down(c, 2)
                if c + 1 < B:
                    transpose_logits(c + 1)
                down(c, 3)

        @block.scalar
        def _(act):
            def aux_hi(block_no, kind, *args):
                act.wait_ge(s_auxfull, block_no + 1)
                bank = ps[:, aux_bank(block_no), :]
                if kind == "xt":
                    b, k = args
                    scale = gain[:, k:k + 1] if b < B else 1.0
                    ins = act.activation(xT[0][:, k, :], bank, ACT.Copy, scale=scale)
                elif kind == "q":
                    pair, = args
                    if pair == 1:
                        act.wait_ge(s_score, 2)
                    for head in (2 * pair - 2, 2 * pair - 1):
                        if head > 0:
                            act.wait_ge(s_stack[head % NSTACK], stack_count(head))
                    ins = act.activation(nat[:, QH, :], bank, ACT.Copy, scale=SCALE)
                elif kind == "k":
                    ins = act.activation(nat[:, KH, :], bank, ACT.Copy)
                elif kind == "v":
                    quad, part = args
                    ins = act.activation(vbuf[:, quad % 2, 2 * part:2 * part + 2, :, 0:DH],
                                         bank.rearrange("p (t h d) -> p t h d", t=2, h=4), ACT.Copy)
                ins.then_inc(s_auxhi, 1)

            def x2_hi(c):
                act.wait_ge(s_fxt, c)
                act.activation(f_xT[0][c % 2][:, :, :], ps[:, PS_XT:PS_XT + 2, :], ACT.Copy).then_inc(s_fxthi, 1)

            def transposed_hi(n):
                head, half = divmod(n, 2)
                dst = pT[0][:, head % 2, :, half * 2 * P:(half + 1) * 2 * P].rearrange(
                    "p k (j q) -> p j k q", j=2)
                for j in range(2):
                    act.wait_ge(s_pt, 2 * n + j + 1)
                    act.activation(dst[:, j], ps[:, PS_PT + j, :].rearrange("p (k q) -> p k q", k=TT),
                                   ACT.Copy).then_inc(s_pthi, 1)

            def gelu(n):
                act.wait_ge(s_up, n + 1)
                if n >= 3:
                    act.wait_ge(s_hlo, n - 2)
                act.activation(f_h[n % 3], ps[:, PS_UP[n % 2], :], ACT.Gelu_apprx_tanh,
                               bias=b1_sb[:, n % FT:n % FT + 1]).then_inc(s_gelu, 1)

            for slot in range(FIRST_SLOT, LAST_SLOT + 1):
                for block_of_aux in aux_at.get(slot, []):
                    if block_of_aux[1] != "out":
                        aux_hi(*block_of_aux)
                if 0 <= slot - 2 < NUNIT:
                    transposed_hi(slot - 2)
                head, part = divmod(slot - 4, 2)
                if part == 1 and 0 <= head < NHEAD:
                    act.wait_ge(s_pv, head + 1)
                    act.activation(vlo_part[:, :], ps[DH:P, PS_OUT, :], ACT.Copy).then_inc(s_vlo, 1)
                n = slot
                if 0 <= n < NUNIT:
                    act.wait_ge(s_max, n + 1)
                    if n >= NPROB:
                        act.wait_ge(s_pt, 2 * (n - NPROB) + 2)
                    for j in range(2):
                        act.activation(prob[:, n % NPROB, j * SEQ:(j + 1) * SEQ],
                                             ps[:, PS_SCORE[n % 2] + j, :], ACT.Exp,
                                             bias=negmax[:, n % 4, j:j + 1], accum_out=rowsum[:, n % 4, j:j + 1])\
                            .then_inc(s_exp, 1)

                for i in weight_slots(slot):
                    wait_weight_loaded(act, i)
                    act.activation(weight_chunk(i)[1][0], weight_stage(i), ACT.Copy).then_inc(s_whi, 1)
                if 0 <= slot - UP_SLOT < TAIL_UPS:
                    gelu(slot - UP_SLOT)

            def copy_logits(c):
                act.wait_ge(s_frm, c + 1)
                act.activation(r_logitT[:, :], ps[0:2 * EXPERTS, PS_ROUTER, :], ACT.Copy).then_inc(s_flt, 1)

            def router_exp(c):
                act.wait_ge(s_frs, c + 1)
                act.activation(r_exp[:, :, :], r_shift[:, :, :], ACT.Exp).then_inc(s_fre, 1)

            copy_logits(0)
            for c in range(B):
                for f in range(TAIL_UPS if c == 0 else 0, FT):
                    gelu(c * FT + f)
                if c == 0:
                    router_exp(0)
                if c + 1 < B:
                    x2_hi(c + 1)
                    copy_logits(c + 1)
                    router_exp(c + 1)

        @block.gpsimd
        def _(pool):
            pool.memset(halves[:, 0, :], 0.5).then_inc(s_half, 1)
            pool.memset(halves[:, 1, :], -0.5).then_inc(s_half, 1)
            pool.wait_ge(s_half, 2)

            def powers(n):
                pool.wait_ge(s_var, n + 1)
                pool.tensor_tensor(ln_pow[:, :, :], ln_var[:, :, :], halves[:, :, :], ALU.pow).then_inc(s_pow, 1)

            def times(dst, src, scalar):
                return pool.tensor_scalar(dst, src, scalar, 1.0, ALU.mult, ALU.mult)

            def hidden_hi(n):
                c, f = divmod(n, FT)
                pool.wait_ge(s_gelu, n + 1)
                if c == 0 and f in (0, TT):
                    pool.wait_ge(s_pv, NHEAD - 1 + f // TT)
                if c >= 1 and f == 0:
                    pool.wait_ge(s_down, 2 * c)
                pool.tensor_scalar(f_hT[0][:, f, :], f_h[n % 3], 1.0, 1.0, ALU.mult, ALU.mult)\
                    .then_inc(s_hhi, 1)

            for slot in range(FIRST_SLOT, LAST_SLOT + 2):
                n = slot - 1
                if 0 <= n < NUNIT:
                    pool.wait_ge(s_inv, n + 1)
                    for j in range(2):
                        p = prob[:, n % NPROB, j * SEQ:(j + 1) * SEQ]
                        times(p, p, rowinv[:, n % 4, j:j + 1]).then_inc(s_prob, 1)
                task = ln_task(slot)
                if task and task[1] == 4:
                    powers(task[0])
                for i in weight_slots(slot):
                    if i in POOL_CHUNKS:
                        pool.wait_ge(s_whi, i + 1)
                        hi_part, lo_part = weight_chunk(i)[1]
                        pool.tensor_tensor(lo_part, weight_stage(i), hi_part, ALU.subtract).then_inc(s_wlo_pool, 1)
                if slot in HIDDEN_SLOTS:
                    hidden_hi(HIDDEN_SLOTS.index(slot))
                pair, r = divmod(slot - 8, 4)
                if r == 0 and 0 <= pair < NPAIR:
                    pool.wait_ge(s_head, 2 * pair + 2)
                    if pair >= NATT:
                        pool.wait_ge(s_aux, aux_index[("out", (pair - NATT) // 4, TT - 1)] + 1)
                    pool.tensor_scalar(attT[0][:, pair % NATT, :], att32[:, :], 1.0, 1.0, ALU.mult, ALU.mult)\
                        .then_inc(s_atthi, 1)
                    pool.wait_ge(s_atthi, pair + 1)
                    pool.tensor_tensor(attT[1][:, pair % NATT, :], att32[:, :], attT[0][:, pair % NATT, :],
                                       ALU.subtract).then_inc(s_att, 1)

            for c in range(B):
                for f in range(len(HIDDEN_SLOTS) if c == 0 else 0, FT):
                    hidden_hi(c * FT + f)
                    if c == 0 and f == TT:
                        powers(B + 1)
                if c + 2 < B:
                    powers(B + c + 2)

        @block.vector
        def _(dve):
            chain = [0]

            def link(ins):
                chain[0] += 1
                ins.then_inc(s_dve, 1)
                dve.wait_ge(s_dve, chain[0])

            def statistics_step(src, t, last):
                ins = dve.bn_stats(ln_stats[:, t, :], src)
                if last:
                    link(ins)
                    for tile in range(TT):
                        ins = dve.bn_aggr(ln_mv[:, tile, :], ln_stats[:, tile, :])
                    link(ins)
                    dve.tensor_copy(ln_var[:, 0, :], ln_mv[:, :, 1])
                    dve.tensor_scalar(ln_var[:, 1, :], ln_mv[:, :, 1], LN_EPS, None, ALU.add).then_inc(s_var, 1)

            def attention_scale():
                root = float(D) ** 0.5
                link(dve.scalar_tensor_tensor(ln_norm[:, 0, :], ln_std, root, ln_rstd,
                                              ALU.mult, ALU.mult))
                link(dve.tensor_scalar(ln_norm[:, 1, :], ln_norm[:, 0, :], RMS_EPS, None, ALU.max))
                link(dve.reciprocal(ln_norm[:, 2, :], ln_norm[:, 1, :]))
                link(dve.scalar_tensor_tensor(ln_scale[:, :], ln_rstd, root, ln_norm[:, 2, :],
                                              ALU.mult, ALU.mult))

            def normalise(dst, src, t, scale):
                return dve.tensor_scalar(dst, src, ln_mv[:, t, 0:1], scale[:, t:t + 1], ALU.subtract, ALU.mult)

            def lo(dst, full, hi, scale=None):
                if scale is None:
                    return dve.tensor_tensor(dst, full, hi, ALU.subtract)
                return dve.scalar_tensor_tensor(dst, full, scale, hi, ALU.mult, ALU.subtract)

            def aux_done(block_no, kind, *args):
                bank = ps[:, aux_bank(block_no), :]
                if kind == "out":
                    half, tile = args
                    dve.wait_ge(s_auxfull, block_no + 1)
                    if half % 2 == 0:
                        dve.wait_ge(s_xres, 16 * (half // 2 + 1))
                    else:
                        dve.wait_ge(s_aux, aux_index[("out", half - 1, tile)] + 1)
                    dve.tensor_tensor(xres[:, tile, :], bank[:, 0:D], xres[:, tile, :], ALU.add)\
                        .then_inc(s_aux, 1)
                    return
                hi_no = sum(1 for k in range(block_no + 1) if aux_kind[k] != "out")
                dve.wait_ge(s_auxhi, hi_no)
                if kind == "xt":
                    k = args[1]
                    scale = gain[:, k:k + 1] if args[0] < B else None
                    ins = lo(xT[1][:, k, :], bank, xT[0][:, k, :], scale)
                elif kind == "q":
                    ins = lo(nat[:, QL, :], bank, nat[:, QH, :], SCALE)
                elif kind == "k":
                    ins = lo(nat[:, KL, :], bank, nat[:, KH, :])
                else:
                    quad, part = args
                    v = vbuf[:, quad % 2, 2 * part:2 * part + 2, :, :]
                    ins = lo(v[:, :, :, DH:2 * DH], bank.rearrange("p (t h d) -> p t h d", t=2, h=4),
                             v[:, :, :, 0:DH])
                ins.then_inc(s_aux, 1)

            aux_kind = [task[0] for task in aux_index]

            def ffn_stats(c, t):
                if t == 0:
                    dve.wait_ge(s_fx1[c % 3], 16 * (c // 3 + 1))
                statistics_step(f_x1[c % 3][:, t, :], t, t == TT - 1)

            def ffn_normalise(c):
                dve.wait_ge(s_pow, B + c + 1)
                if c >= 2:
                    dve.wait_ge(s_fxt, c - 1)
                for t in range(TT):
                    ins = normalise(f_x2[:, t, :], f_x1[c % 3][:, t, :], t, ln_rstd)
                ins.then_inc(s_fx2, 1)

            def ffn_split(c):
                dve.wait_ge(s_fxthi, c)
                lo(f_xT[1][c % 2][:, :, :], ps[:, PS_XT:PS_XT + 2, :], f_xT[0][c % 2][:, :, :]).then_inc(s_fxtlo, 1)

            def transposed_lo(n):
                head, half = divmod(n, 2)
                part = [p[:, head % 2, :, half * 2 * P:(half + 1) * 2 * P].rearrange(
                    "p k (j q) -> p j k q", j=2) for p in pT]
                for j in range(2):
                    dve.wait_ge(s_pthi, 2 * n + j + 1)
                    lo(part[1][:, j], ps[:, PS_PT + j, :].rearrange("p (k q) -> p k q", k=TT),
                       part[0][:, j]).then_inc(s_ptlo, 1)

            def hidden_lo(n):
                dve.wait_ge(s_hhi, n + 1)
                lo(f_hT[1][:, n % FT, :], f_h[n % 3], f_hT[0][:, n % FT, :]).then_inc(s_hlo, 1)

            for slot in range(FIRST_SLOT, LAST_SLOT + 1):
                n = slot
                if 0 <= n < NUNIT:
                    dve.wait_ge(s_score, n + 1)
                    dve.tensor_reduce(negmax[:, n % 4, :], ps[:, PS_SCORE[n % 2]:PS_SCORE[n % 2] + 2, :],
                                      AX.X, ALU.max, negate=True).then_inc(s_max, 1)
                n = slot - 1
                if 0 <= n < NUNIT:
                    dve.wait_ge(s_exp, 2 * n + 2)
                    dve.reciprocal(rowinv[:, n % 4, :], rowsum[:, n % 4, :]).then_inc(s_inv, 1)
                early, late = aux_of(slot)
                for block_of_aux in early:
                    aux_done(*block_of_aux)
                if 0 <= slot - 2 < NUNIT:
                    transposed_lo(slot - 2)
                head, part = divmod(slot - 4, 2)
                if part == 1 and 0 <= head < NHEAD:
                    dve.wait_ge(s_vlo, head + 1)
                    if head >= 2 and head % 2 == 0:
                        dve.wait_ge(s_att, head // 2)
                    dve.tensor_tensor(att32[head % 2 * DH:(head % 2 + 1) * DH, :], ps[0:DH, PS_OUT, :],
                                      vlo_part[:, :], ALU.add).then_inc(s_head, 1)
                for block_of_aux in late:
                    aux_done(*block_of_aux)
                if slot in HIDDEN_SLOTS:
                    hidden_lo(HIDDEN_SLOTS.index(slot))
                for i in weight_slots(slot):
                    if i in POOL_CHUNKS:
                        continue
                    dve.wait_ge(s_whi, i + 1)
                    hi_part, lo_part = weight_chunk(i)[1]
                    lo(lo_part, weight_stage(i), hi_part).then_inc(s_wlo, 1)
                task = ln_task(slot)
                if task:
                    b, step = task
                    xb = xin[:, :, :]
                    if step == 0 and b == B:
                        dve.wait_ge(s_fx1[0], 16)
                    elif step == 0:
                        dve.wait_ge(s_x, 16 * (b + 1))
                    if step < 4:
                        statistics_step(xb[:, step, :], step, step == 3)
                    elif step == 6 and b == B:
                        ffn_normalise(0)
                    elif step == 5 and b < B:
                        dve.wait_ge(s_pow, b + 1)
                        attention_scale()
                        if b == 0:
                            dve.wait_ge(s_const, 16 * N_CONST)
                            dve.tensor_scalar(gain[:, :], gamma_sb[:, :], 1.0, None, ALU.add)
                    elif step == 8 and b == B:
                        dve.wait_ge(s_router, 16 * (KT + 1))
                        link(dve.tensor_copy(rw_parts[:, :, 0:EXPERTS], rw_sb[:, :, :]))
                        link(lo(rw_parts[:, :, EXPERTS:], rw_sb[:, :, :], rw_parts[:, :, 0:EXPERTS]))
                    elif step in (6, 8) and b < B:
                        for t in (step - 6, step - 5):
                            ins = normalise(xn[:, t, :], xb[:, t, :], t, ln_scale)
                        if step == 8:
                            ins.then_inc(s_xn, 1)

            def routing_shift(c):
                dve.wait_ge(s_frt, c + 1)
                logits = ps[:, PS_ROUTER, 0:TT * 2 * EXPERTS].rearrange("p (t e) -> p t e", t=TT)
                link(dve.tensor_copy(r_half[:, :, :], logits[:, :, EXPERTS:]))
                link(dve.tensor_tensor(r_logit[:, :, :], logits[:, :, 0:EXPERTS], r_half[:, :, :], ALU.add))
                link(dve.tensor_reduce(r_max[:, :], r_logit[:, :, :], AX.X, ALU.max))
                dve.tensor_tensor(r_shift[:, :, :], r_logit[:, :, :],
                                  r_max[:, :].unsqueeze(2).broadcast_to((P, TT, EXPERTS)),
                                  ALU.subtract).then_inc(s_frs, 1)

            def routing_weight(c):
                dve.wait_ge(s_fre, c + 1)
                link(dve.reduce_sum(r_sum[:, :], r_exp[:, :, :], AX.X))
                link(dve.reciprocal(r_inv[:, :], r_sum[:, :]))
                link(dve.tensor_tensor(r_prob[:, :, :], r_exp[:, :, :],
                                       r_inv[:, :].unsqueeze(2).broadcast_to((P, TT, EXPERTS)), ALU.mult))
                for t in range(TT):
                    ins = dve.max(r_top[:, t, :], r_prob[:, t, :])
                link(ins)
                link(dve.tensor_tensor(r_tsum[:, :], r_top[:, :, 0], r_top[:, :, 1], ALU.add))
                link(dve.reciprocal(r_tinv[:, :], r_tsum[:, :]))
                link(dve.tensor_tensor(r_pair[:, :, :], r_top[:, :, 0:2],
                                       r_tinv[:, :].unsqueeze(2).broadcast_to((P, TT, 2)), ALU.mult))
                link(dve.tensor_tensor(r_weight[:, c % 2, :], r_pair[:, :, 0], r_pair[:, :, 1], ALU.add))

            def finish(c, part):
                if c == 0 and part == 0:
                    dve.wait_ge(s_b2, 16)
                dve.wait_ge(s_down, 2 * c + part + 1)
                if part == 0 and c >= 2:
                    dve.wait_ge(s_out[c % 2], 32 * (c // 2))
                y = f_y[:, part]
                dve.tensor_tensor(y, ps[:, PS_DOWN[part], :].rearrange("p (t d) -> p t d", t=2),
                                  b2_sb[:, :].unsqueeze(1).broadcast_to((P, 2, D)), ALU.add).then_inc(s_fy, 1)
                dve.wait_ge(s_fy, 2 * c + part + 1)
                for t in range(2):
                    tile = 2 * part + t
                    ins = dve.scalar_tensor_tensor(f_o[:, c % 2, tile, :], y[:, t, :],
                                                   r_weight[:, c % 2, tile:tile + 1],
                                                   f_x1[c % 3][:, tile, :], ALU.mult, ALU.add)
                ins.then_inc(s_fo, 1)

            for c in range(B):
                first = len(HIDDEN_SLOTS) if c == 0 else 0
                for f in range(first, FT):
                    hidden_lo(c * FT + f)
                    if c == 0 and f in (2, 3):
                        for t in (0, 1):
                            ffn_stats(1, 2 * (f - 2) + t)
                    if c == 0 and f == 4:
                        routing_shift(0)
                if c == 0:
                    ffn_normalise(1)
                    for block_of_out in last_out:
                        aux_done(*block_of_out)
                    routing_weight(0)
                if c + 1 < B:
                    ffn_split(c + 1)
                if c + 2 < B:
                    for t in range(TT):
                        ffn_stats(c + 2, t)
                    ffn_normalise(c + 2)
                if c + 1 < B:
                    routing_shift(c + 1)
                finish(c, 0)
                if c + 1 < B:
                    routing_weight(c + 1)
                finish(c, 1)


def kernel(**inputs):
    import numpy as np
    import concourse.bacc as bacc
    from concourse.bass_utils import run_bass_kernel_spmd

    get = lambda name: np.asarray(inputs[name])
    arrays = {
        "x": get("L0_attn_x"),
        "gamma_cols": np.ascontiguousarray(get("L0_attn_gamma").reshape(KT, P).T),
        "w_qkv": get("L0_attn_w_qkv"),
        "w_out": get("L0_attn_w_out"),
        "router_w": get("L0_ffn_router_w"),
        "w1": get("L0_ffn_w1"),
        "b1_cols": np.ascontiguousarray(get("L0_ffn_b1").reshape(FT, P).T),
        "w2": get("L0_ffn_w2"),
        "b2_rows": np.ascontiguousarray(np.broadcast_to(get("L0_ffn_b2"), (P, D))),
        "ident": np.eye(P, dtype=np.float32),
    }
    arrays = {f"in_{k}": np.ascontiguousarray(v) for k, v in arrays.items()}
    nc = bacc.Bacc("TRN2", target_bir_lowering=False, num_devices=1)
    args = [nc.dram_tensor(k, v.shape, mybir.dt.from_np(v.dtype), kind="ExternalInput").ap()
            for k, v in arrays.items()]
    out = nc.dram_tensor("out_y", (B, SEQ, D), F32, kind="ExternalOutput").ap()
    layer_kernel(nc, *args, out)
    result = run_bass_kernel_spmd(nc, [arrays], core_ids=[0])
    return result.results[0]["out_y"]
```
